# Optimizing a Trainium2 kernel written in Bass

```python
import numpy as np
import jax
import jax.numpy as jnp

def _softmax(x, axis=-1):
    return jax.nn.softmax(x, axis=axis)

def _gelu(x):
    return jax.nn.gelu(x, approximate=True)

def _silu(x):
    return jax.nn.silu(x)

def _sigmoid(x):
    return jax.nn.sigmoid(x)

def _layernorm(x, axis=-1, eps=1e-05):
    m = jnp.mean(x, axis=axis, keepdims=True)
    v = jnp.var(x, axis=axis, keepdims=True)
    return (x - m) / jnp.sqrt(v + eps)

def _scatter_add(tgt, idx, src, axis=0):
    return tgt.at[idx].add(src)

def _segment_sum(src, seg, n):
    return jax.ops.segment_sum(src, seg, n)
kernel_name = 'mk_audio_tower_d1_tok_audfeat512_r4_609c73'

def setup_inputs(seed: int=0):
    np.random.seed(seed)
    _w = jnp.asarray

    def _rec_inputs():
        import jax
        import jax.numpy as jnp
        _rk = jax.random.key(seed)
        x = -0.00190633 + 1.00279 * jax.random.normal(jax.random.fold_in(_rk, 1), (128, 64, 7), jnp.float32)
        return x
    x = _rec_inputs()

    def _L0_tok_setup():
        import jax, jax.numpy as jnp
        import numpy as np
        SIG_DEPTH = 4

        def _outer(a, b):
            return (a[:, :, None] * b[:, None, :]).reshape(a.shape[0], -1)
        key = jax.random.key(seed)
        k1, k2 = jax.random.split(key)
        B, L, Cin = (64, 64, 7)
        out_dim = 128
        C = Cin + 1
        sig_channels = sum((C ** k for k in range(1, SIG_DEPTH + 1)))
        inp = jax.random.normal(k1, (B, L, Cin), dtype=jnp.float32)
        W = jax.random.normal(k2, (out_dim, sig_channels), dtype=jnp.float32) * 0.02
        b = jnp.zeros((out_dim,), dtype=jnp.float32)
        return {'inp': inp, 'W': W, 'b': b}
    _L0_tok_all = _L0_tok_setup()
    _L0_tok_in = {k: v for k, v in _L0_tok_all.items() if k in ('W', 'b')}
    del _L0_tok_all

    def _L0_attn_setup():
        import jax, jax.numpy as jnp
        import numpy as np
        B, N, D_IN, D_HID, D_OUT = (8, 512, 128, 128, 128)
        key = jax.random.key(seed)
        k1, k2, k3, k4 = jax.random.split(key, 4)
        x = jax.random.normal(k1, (B, N, D_IN), dtype=jnp.float32)
        s_in = 1.0 / np.sqrt(D_IN)
        s_hid = 1.0 / np.sqrt(D_HID)
        Wq = jax.random.uniform(k2, (D_HID, D_IN), minval=-s_in, maxval=s_in, dtype=jnp.float32)
        Wk = jax.random.uniform(k3, (D_HID, D_IN), minval=-s_in, maxval=s_in, dtype=jnp.float32)
        Wv = jax.random.uniform(k4, (D_OUT, D_HID), minval=-s_hid, maxval=s_hid, dtype=jnp.float32)
        return {'x': x, 'Wq': Wq, 'Wk': Wk, 'Wv': Wv}
    _L0_attn_all = _L0_attn_setup()
    _L0_attn_in = {k: v for k, v in _L0_attn_all.items() if k in ('Wq', 'Wk', 'Wv')}
    del _L0_attn_all

    def _L0_ffn_setup():
        import jax, jax.numpy as jnp
        import numpy as np
        DIM = 128
        INTER = 64
        SHARED_INTER = 256
        N_EXPERTS = 64
        TOP_K = 6
        key = jax.random.key(seed)
        ks = jax.random.split(key, 8)
        s = 0.05
        return {'x': jax.random.normal(ks[0], (2, 128, DIM), jnp.float32), 'w_gate': jax.random.normal(ks[1], (N_EXPERTS, DIM), jnp.float32) * s, 'w1': jax.random.normal(ks[2], (N_EXPERTS, INTER, DIM), jnp.float32) * s, 'w2': jax.random.normal(ks[3], (N_EXPERTS, INTER, DIM), jnp.float32) * s, 'w3': jax.random.normal(ks[4], (N_EXPERTS, INTER, DIM), jnp.float32) * s, 'w_sg': jax.random.normal(ks[5], (SHARED_INTER, DIM), jnp.float32) * s, 'w_su': jax.random.normal(ks[6], (SHARED_INTER, DIM), jnp.float32) * s, 'w_sd': jax.random.normal(ks[7], (DIM, SHARED_INTER), jnp.float32) * s}
    _L0_ffn_all = _L0_ffn_setup()
    _L0_ffn_in = {k: v for k, v in _L0_ffn_all.items() if k in ('w_gate', 'w1', 'w2', 'w3', 'w_sg', 'w_su', 'w_sd')}
    del _L0_ffn_all
    return {'x': x, 'L0_tok_W': _L0_tok_in['W'], 'L0_tok_b': _L0_tok_in['b'], 'L0_attn_Wq': _L0_attn_in['Wq'], 'L0_attn_Wk': _L0_attn_in['Wk'], 'L0_attn_Wv': _L0_attn_in['Wv'], 'L0_ffn_w_gate': _L0_ffn_in['w_gate'], 'L0_ffn_w1': _L0_ffn_in['w1'], 'L0_ffn_w2': _L0_ffn_in['w2'], 'L0_ffn_w3': _L0_ffn_in['w3'], 'L0_ffn_w_sg': _L0_ffn_in['w_sg'], 'L0_ffn_w_su': _L0_ffn_in['w_su'], 'L0_ffn_w_sd': _L0_ffn_in['w_sd']}

def reference(x, L0_tok_W, L0_tok_b, L0_attn_Wq, L0_attn_Wk, L0_attn_Wv, L0_ffn_w_gate, L0_ffn_w1, L0_ffn_w2, L0_ffn_w3, L0_ffn_w_sg, L0_ffn_w_su, L0_ffn_w_sd):
    import jax
    import jax.numpy as jnp

    def _L0_tok_ref(inp, W, b):
        import jax, jax.numpy as jnp
        import numpy as np
        SIG_DEPTH = 4

        def _outer(a, b):
            return (a[:, :, None] * b[:, None, :]).reshape(a.shape[0], -1)
        B, L, Cin = inp.shape
        t = jnp.broadcast_to(jnp.linspace(0.0, 1.0, L, dtype=inp.dtype)[None, :, None], (B, L, 1))
        x = jnp.concatenate([t, inp], axis=-1)
        C = Cin + 1
        d = SIG_DEPTH
        dx = jnp.transpose(x[:, 1:] - x[:, :-1], (1, 0, 2))
        init = tuple((jnp.zeros((B, C ** (k + 1)), x.dtype) for k in range(d)))

        def step(levels, v):
            e = [v]
            for k in range(1, d):
                e.append(_outer(e[-1], v) / (k + 1))
            new = []
            for k in range(d):
                acc = levels[k] + e[k]
                for i in range(k):
                    acc = acc + _outer(levels[i], e[k - 1 - i])
                new.append(acc)
            sig = jnp.concatenate(new, axis=-1)
            return (tuple(new), sig)
        _, sigs = jax.lax.scan(step, init, dx)
        sigs = jnp.transpose(sigs, (1, 0, 2))
        return sigs @ W.T + b

    def _L0_attn_ref(x, Wq, Wk, Wv):
        import jax, jax.numpy as jnp
        import numpy as np
        B, N, D_IN, D_HID, D_OUT = (8, 512, 128, 128, 128)
        q = jnp.einsum('bnd,hd->bnh', x, Wq)
        k = jnp.einsum('bnd,hd->bnh', x, Wk)
        v = jnp.einsum('bnd,od->bno', x, Wv)
        scores = jnp.einsum('bqh,bkh->bqk', q, k)
        attn = jax.nn.softmax(scores, axis=1)
        return jnp.einsum('bqk,bko->bqo', attn, v)

    def _L0_ffn_ref(x, w_gate, w1, w2, w3, w_sg, w_su, w_sd):
        import jax, jax.numpy as jnp
        import numpy as np
        DIM = 128
        INTER = 64
        SHARED_INTER = 256
        N_EXPERTS = 64
        TOP_K = 6
        orig_shape = x.shape
        xf = x.reshape(-1, x.shape[-1])
        T = xf.shape[0]
        scores = xf @ w_gate.T
        top_vals, top_idx = jax.lax.top_k(scores, TOP_K)
        expert_weights = jax.nn.softmax(top_vals, axis=-1)
        comb = jnp.zeros(scores.shape, xf.dtype).at[jnp.arange(T)[:, None], top_idx].set(expert_weights)
        x1 = jax.nn.silu(jnp.einsum('td,eid->tei', xf, w1))
        x3 = jnp.einsum('td,eid->tei', xf, w3)
        y = jnp.einsum('tei,eid->ted', x1 * x3, w2)
        routed = jnp.einsum('ted,te->td', y, comb)
        shared = jax.nn.silu(xf @ w_sg.T) * (xf @ w_su.T) @ w_sd.T
        return (routed + shared).reshape(orig_shape)
    h = _L0_tok_ref(x, L0_tok_W, L0_tok_b)
    h = h + _L0_attn_ref(_layernorm(h, axis=-1), L0_attn_Wq, L0_attn_Wk, L0_attn_Wv)
    h = h + _L0_ffn_ref(_layernorm(h, axis=-1), L0_ffn_w_gate, L0_ffn_w1, L0_ffn_w2, L0_ffn_w3, L0_ffn_w_sg, L0_ffn_w_su, L0_ffn_w_sd)
    return h

_drawn_inputs = setup_inputs


def setup_inputs(seed=0):
    import zlib

    import numpy as np

    out = dict(_drawn_inputs(seed))
    spreads = {'L0_tok_b': (0.0, 0.46)}
    factors = {'L0_ffn_w_gate': 8.0,
     'L0_ffn_w1': 8.0,
     'L0_ffn_w2': 8.0,
     'L0_ffn_w3': 8.0,
     'L0_ffn_w_sg': 5.745,
     'L0_ffn_w_su': 5.589,
     'L0_ffn_w_sd': 5.61}
    for name, (base, spread) in spreads.items():
        noise = np.random.default_rng([zlib.crc32(name.encode()), seed]).standard_normal(out[name].shape)
        drawn = base * np.exp(spread * noise) if base else spread * noise
        out[name] = jnp.asarray(drawn.astype(out[name].dtype))
    for name, factor in factors.items():
        out[name] = (out[name] * factor).astype(out[name].dtype)
    return out
```

```python
from contextlib import ExitStack

import concourse.bass as bass
from concourse import mybir

F32 = mybir.dt.float32
F32R = mybir.dt.float32r
ALU = mybir.AluOpType
ACT = mybir.ActivationFunctionType
AX_X = mybir.AxisListType.X

P = 128
NB = 128
T = 63
C = 8
D = 128
NE = 64
TOPK = 6
KT = C ** 3 // P
K5 = C * C + C + 1
NU = C * D
RING = 3
HALVES = 2
GB = 8
NG = NB // GB
PT = GB // 2
TP = 64
GT = GB * T
TT = 2 * T
NQ = 2 + NE // 2
WCOLS = 3 * NQ * P
CHUNKS = 16
CH = WCOLS // CHUNKS
EPS = 1e-5
SENTINEL = 3.0e38
O_C, O_ONE, O_V, O_VH, O_VT, O_E1, O_D1 = 64, 72, 73, 81, 89, 97, 105
SLOT = 113
PK = SLOT - 64
N_DV = 47


def audio_tower(nc, x, tgrid, wt, bias, wq, wk, wvt, wgt, ffw, out):
    h_dram = nc.dram_tensor("h_tokens", (NB, T, D), F32).ap()
    h_load = h_dram.rearrange("(g p b) t o -> g b t p o", p=PT, b=2)
    out_rows = out.rearrange("(g p r) o -> g r p o", p=PT, r=TT)

    with ExitStack() as ctx:
        def sem(name):
            return ctx.enter_context(nc.semaphore(name))

        def sb(name, shape, dt=F32, scope=ctx):
            return scope.enter_context(nc.sbuf_tensor(name, shape, dt))

        ident = sb("ident", [P, P])
        ident2 = sb("ident2", [P, NE])
        w_hi = sb("w_hi", [P, WCOLS], F32R)
        w_lo = sb("w_lo", [P, WCOLS], F32R)
        wq_sb = sb("wq_sb", [P, D])
        wk_sb = sb("wk_sb", [P, D])
        wv_sb = sb("wv_sb", [P, D])
        wg_sb = sb("wg_sb", [P, NE])
        qk_sb = sb("qk_sb", [P, D])
        s1 = ExitStack()
        p1 = ExitStack()
        ws_hi = sb("ws_hi", [P, KT + 1, NU], F32R, s1)
        ws_lo = sb("ws_lo", [P, KT + 1, NU], F32R, s1)
        ws_raw = sb("ws_raw", [P, 2, NU], F32, s1)
        x_sb = sb("x_sb", [P, T + 1, C - 1], F32, s1)
        t_sb = sb("t_sb", [P, T + 1], F32, s1)
        s1_sb = sb("s1_sb", [P, T, C], F32, s1)
        steps = sb("steps", [P, T, PK], F32, s1)
        slot = sb("slot", [P, RING, SLOT], F32, s1)
        s2r = sb("s2r", [P, RING, C * C], F32, s1)
        s3r = sb("s3r", [P, RING, C ** 3], F32, s1)
        small = sb("small", [P, 4, C * C], F32, s1)
        b3 = sb("b3", [P, C ** 3], F32, s1)
        e3 = sb("e3", [P, C ** 3], F32, s1)
        a_sb = sb("a_sb", [P, C ** 3], F32, s1)
        at_hi = sb("at_hi", [P, RING, KT + 1, NB], F32R, s1)
        at_lo = sb("at_lo", [P, RING, KT + 1, NB], F32R, s1)
        h_sb = sb("h_sb", [P, RING, D], F32, s1)
        chunk = sb("chunk", [P, CH], F32, s1)
        u_ps = p1.enter_context(nc.psum_tensor("u_ps", [P, RING, HALVES, NU // HALVES], F32))
        ta_ps = p1.enter_context(nc.psum_tensor("ta_ps", [P, C ** 3], F32))
        t5_ps = p1.enter_context(nc.psum_tensor("t5_ps", [P, 512], F32))
        s1.close()
        p1.close()
        h_tok = sb("h_tok", [P, PT, D])
        st = sb("st", [P, PT, 6])
        mv = sb("mv", [P, PT, 2])
        vare = sb("vare", [P, PT])
        rstd = sb("rstd", [P, PT])
        mhalf = sb("mhalf", [P, PT])
        eps = sb("eps", [P, PT])
        xn = sb("xn", [P, PT, D])
        xnT = sb("xnT", [P, PT, P])
        pT = sb("pT", [P, PT, P])
        att = sb("att", [P, PT, P])
        mx = sb("mx", [P, PT])
        sm = sb("sm", [P, PT])
        rs = sb("rs", [P, PT])
        v_sb = sb("v_sb", [P, PT, D])
        h2 = sb("h2", [P, PT, D])
        x2n = sb("x2n", [P, GT])
        h2T = sb("h2T", [P, GT])
        combT = sb("combT", [P, GT])
        score = sb("score", [P, PT, NE + 2])
        taken = sb("taken", [P, PT, NE + 2])
        top = sb("top", [P, PT, 8])
        ex = sb("ex", [P, PT, NE])
        mask = sb("mask", [P, PT, NE])
        spare = sb("spare", [P, 4])
        gsum = sb("gsum", [P, PT])
        grs = sb("grs", [P, PT])
        comb = sb("comb", [P, PT, 2, NE])
        expand = sb("expand", [P, NE, NE], F32R)
        x_hi = sb("x_hi", [P, GT], F32R)
        x_lo = sb("x_lo", [P, GT], F32R)
        c_st = sb("c_st", [P, GT], F32R)
        sig = sb("sig", [P, 2, GT])
        gat = sb("gat", [P, 2, GT])
        hid = sb("hid", [P, 2, GT])
        hid_hi = sb("hid_hi", [P, 2, GT], F32R)
        hid_lo = sb("hid_lo", [P, 2, GT], F32R)
        yT = sb("yT", [P, GT])
        y_sb = sb("y_sb", [P, PT, D])
        x1_ps = ctx.enter_context(nc.psum_tensor("x1_ps", [P, 2, 512], F32))
        x3_ps = ctx.enter_context(nc.psum_tensor("x3_ps", [P, 2, 512], F32))
        cb_ps = ctx.enter_context(nc.psum_tensor("cb_ps", [P, 512], F32))
        y_ps = ctx.enter_context(nc.psum_tensor("y_ps", [P, 512], F32))
        pa = ctx.enter_context(nc.psum_tensor("pa", [P, 512], F32))
        pb = ctx.enter_context(nc.psum_tensor("pb", [P, 512], F32))

        s_in = sem("s_in")
        s_wqk = sem("s_wqk")
        s_raw = [sem("s_raw0"), sem("s_raw1")]
        s_rawhi = sem("s_rawhi")
        s_rawlo = sem("s_rawlo")
        s_chunk = sem("s_chunk")
        s_chi = sem("s_chi")
        s_clo = sem("s_clo")
        s_id = sem("s_id")
        s_exp = sem("s_exp")
        s_pre = sem("s_pre")
        s_slot = sem("s_slot")
        s_pool = sem("s_pool")
        s_b = sem("s_b")
        s_s2 = sem("s_s2")
        s_s3 = sem("s_s3")
        s_e = sem("s_e")
        s_a = sem("s_a")
        s_ta = sem("s_ta")
        s_athi = sem("s_athi")
        s_atlo = sem("s_atlo")
        s_u = sem("s_u")
        s_acc = sem("s_acc")
        s_hst = [sem(f"s_hst{j}") for j in range(RING)]
        s_load = sem("s_load")
        s_dv = sem("s_dv")
        s_rstd = sem("s_rstd")
        s_veps = sem("s_veps")
        s_pe = sem("s_pe")
        s_ac = sem("s_ac")
        s_zero = sem("s_zero")
        s_qk = sem("s_qk")
        s_xhi = sem("s_xhi")
        s_xlo = sem("s_xlo")
        s_chi2 = sem("s_chi2")
        s_clo2 = sem("s_clo2")
        s_x1 = sem("s_x1")
        s_x3 = sem("s_x3")
        s_cb = sem("s_cb")
        s_y = sem("s_y")
        s_silu = sem("s_silu")
        s_g = sem("s_g")
        s_h = sem("s_h")
        s_hi = sem("s_hi")
        s_lo = sem("s_lo")
        s_yadd = sem("s_yadd")
        s_yt = sem("s_yt")
        s_yc = sem("s_yc")
        s_h2t = sem("s_h2t")
        s_h2c = sem("s_h2c")
        s_out = sem("s_out")

        def after(eng, s, value):
            if not isinstance(value, int) or value > 0:
                eng.wait_ge(s, value)

        def wait_apart(eng, s, value, place):
            eng.wait_ge(s, value)
            nc.vector.memset(spare[:, place:place + 1], 0.0)

        def steps_of_stage1(eng, body, prep=None):
            with eng.Fori(0, CHUNKS) as i:
                if prep:
                    prep(i)
                for j in range(RING):
                    body(i, j, i * RING + j, False)
            with eng.Fori(0, T // RING - 1 - CHUNKS) as n:
                i = n + CHUNKS
                for j in range(RING):
                    body(i, j, i * RING + j, False)
            i = T // RING - 1
            for j in range(RING):
                body(i, j, i * RING + j, True)

        block = ctx.enter_context(nc.Block())

        @block.sync
        def _(sp):
            sp.dma_start(x_sb[:].rearrange("p t c -> p (t c)"), x).then_inc(s_in, 16)
            sp.dma_start(t_sb[:], tgrid.to_broadcast([P, T + 1])).then_inc(s_in, 16)
            sp.dma_start(h_sb[:, RING - 1, :], bias.to_broadcast([P, D])).then_inc(s_in, 16)
            w4 = wt[C + C * C + C ** 3:, :].rearrange("(k p l) o -> k p (l o)", k=KT, l=C)
            for k in range(KT + 1):
                if k >= 2:
                    sp.wait_ge(s_rawlo, k - 1)
                if k < KT:
                    sp.dma_start(ws_raw[:, k % 2, :], w4[k]).then_inc(s_raw[k % 2], 16)
                else:
                    for r0, n, w0 in ((0, C * C, C + C * C), (C * C, C, C), (C * C + C, 1, 0)):
                        sp.dma_start(
                            ws_raw[r0:r0 + n, k % 2, :],
                            wt[w0:w0 + n * C, :].rearrange("(p l) o -> p (l o)", l=C),
                        ).then_inc(s_raw[k % 2], 16)
            sp.dma_start(wq_sb[:], wq).then_inc(s_wqk, 16)
            sp.dma_start(wk_sb[:], wk).then_inc(s_wqk, 16)
            sp.dma_start(wv_sb[:], wvt).then_inc(s_wqk, 16)
            sp.dma_start(wg_sb[:], wgt).then_inc(s_wqk, 16)

            def load_chunk(i):
                sp.wait_ge(s_clo, i)
                sp.dma_start(chunk[:], ffw[:, bass.ds(i * CH, CH)]).then_inc(s_chunk, 16)

            def store_h(i, j, t, last):
                sp.wait_ge(s_acc, (t + 1) * C)
                sp.dma_start(h_dram[:, t, :], h_sb[:, j, :]).then_inc(s_hst[j], 16)

            steps_of_stage1(sp, store_h, load_chunk)

            def load_group(g):
                for b in range(2):
                    sp.dma_start(h_tok[b * TP:b * TP + T, :, :], h_load[g, b]).then_inc(s_load, 16)

            for j in range(RING):
                sp.wait_ge(s_hst[j], 16 * (T // RING))
            sp.wait_ge(s_zero, 1)
            load_group(0)
            sp.wait_ge(s_dv, DV["h2"])
            load_group(1)
            with sp.Fori(0, NG - 2) as g:
                sp.wait_ge(s_dv, (g + 1) * N_DV + DV["h2"])
                load_group(g + 2)
                sp.wait_ge(s_yc, g + 1)
                sp.dma_start(out_rows[g], y_sb[0:TT, :, :]).then_inc(s_out, 16)
            for g in range(NG - 2, NG):
                sp.wait_ge(s_yc, g + 1)
                sp.dma_start(out_rows[g], y_sb[0:TT, :, :]).then_inc(s_out, 16)
            sp.wait_ge(s_out, 16 * NG)

        @block.gpsimd
        def _(pool):
            nc.gpsimd.memset(ident[:], 0.0).then_inc(s_id, 1)
            pool.wait_ge(s_id, 1)
            nc.gpsimd.affine_select(out=ident[:], in_=ident[:], compare_op=ALU.not_equal, fill=1.0, base=0,
                                    pattern=[[-1, P]], channel_multiplier=1).then_inc(s_id, 1)
            nc.gpsimd.memset(ident2[:], 0.0).then_inc(s_id, 1)
            for b in range(2):
                pool.wait_ge(s_id, 3 + b)
                nc.gpsimd.affine_select(out=ident2[:], in_=ident2[:], compare_op=ALU.not_equal, fill=1.0,
                                        base=-b * NE, pattern=[[-1, NE]], channel_multiplier=1).then_inc(s_id, 1)
            nc.gpsimd.memset(s2r[:, 0, :], 0.0).then_inc(s_s2, 1)
            nc.gpsimd.memset(s3r[:, 0, :], 0.0).then_inc(s_s3, 1)
            pool.wait_ge(s_pre, N_PRE)

            def outer(o, a, b, na):
                nb = b.shape[-1]
                return nc.gpsimd.tensor_tensor(
                    o.rearrange("p (a b) -> p a b", a=na),
                    a.unsqueeze(2).to_broadcast([P, na, nb]),
                    b.unsqueeze(1).to_broadcast([P, na, nb]), ALU.mult)

            def state(i, j, t, last):
                nx = (j + 1) % RING
                s = slot[:, j, :]
                after(pool, s_acc, (t - RING + 1) * C if not isinstance(t, int) or t >= RING else 0)
                nc.gpsimd.tensor_copy(s[:, 64:SLOT], steps[:, t, :]).then_inc(s_slot, 1)
                pool.wait_ge(s_slot, t + 1)
                outer(small[:, 0, :], s[:, O_D1:O_D1 + C], s[:, O_VH:O_VH + C], C).then_inc(s_pool, 1)
                outer(small[:, 1, :], s[:, O_C:O_C + C], s[:, O_V:O_V + C], C).then_inc(s_pool, 1)
                pool.wait_ge(s_pool, 3 * t + 1)
                pool.wait_ge(s_s2, t + 1)
                nc.gpsimd.tensor_tensor(s[:, 0:64], s2r[:, j, :], small[:, 0, :], ALU.add).then_inc(s_b, 1)
                pool.wait_ge(s_pool, 3 * t + 2)
                pool.wait_ge(s_a, t - 1) if not isinstance(t, int) or t > 1 else None
                nc.gpsimd.tensor_tensor(s2r[:, nx, :], s2r[:, j, :], small[:, 1, :], ALU.add).then_inc(s_s2, 1)
                pool.wait_ge(s_b, t + 1)
                outer(b3[:], s[:, 0:64], s[:, O_V:O_V + C], C * C).then_inc(s_pool, 1)
                pool.wait_ge(s_pool, 3 * t + 3)
                pool.wait_ge(s_s3, t + 1)
                nc.gpsimd.tensor_tensor(s3r[:, nx, :], s3r[:, j, :], b3[:], ALU.add).then_inc(s_s3, 1)

            def split_chunk(i):
                pool.wait_ge(s_chi, i + 1)
                nc.gpsimd.tensor_tensor(w_lo[:, bass.ds(i * CH, CH)], chunk[:],
                                        w_hi[:, bass.ds(i * CH, CH)].bitcast(F32), ALU.subtract).then_inc(s_clo, 1)

            for t in range(2):
                state(0, t, t, False)
            state(0, 2, 2, False)
            split_chunk(0)
            with pool.Fori(0, CHUNKS - 1) as n:
                i = n + 1
                for j in range(RING):
                    state(i, j, i * RING + j, False)
                split_chunk(i)
            with pool.Fori(0, T // RING - CHUNKS) as n:
                i = n + CHUNKS
                for j in range(RING):
                    state(i, j, i * RING + j, False)

            pool.wait_ge(s_zero, 1)

            def inverse_std(g, norm):
                pool.wait_ge(s_dv, g * N_DV + DV["var1" if norm == 0 else "var2"])
                nc.gpsimd.tensor_tensor(vare[:], mv[:, :, 1], eps[:], ALU.add).then_inc(s_veps, 1)
                pool.wait_ge(s_veps, g * 2 + norm + 1)
                nc.gpsimd.tensor_tensor(rstd[:], vare[:], mhalf[:], ALU.pow).then_inc(s_rstd, 1)

            def low_part(g, q):
                n = g * NQ + q
                pool.wait_ge(s_hi, n + 1)
                after(pool, s_y, n - 1)
                nc.gpsimd.tensor_tensor(hid_lo[:, q % 2, :], hid[:, q % 2, :],
                                        hid_hi[:, q % 2, :].bitcast(F32), ALU.subtract).then_inc(s_lo, 1)

            def round_(g, attention):
                for q in range(2, NQ):
                    low_part(g, q - 1)
                    if attention and q == 2 + RUN["rstd1"]:
                        inverse_std(g + 1, 0)
                    if attention and q == 2 + RUN["rstd2"]:
                        inverse_std(g + 1, 1)

            inverse_std(0, 0)
            inverse_std(0, 1)
            pool.wait_ge(s_rstd, 2)
            nc.gpsimd.tensor_copy(expand[:], ident2[:].unsqueeze(2).to_broadcast([P, NE, NE])).then_inc(s_exp, 1)
            low_part(0, 0)
            with pool.Fori(0, NG - 1) as g:
                round_(g, True)
                low_part(g, NQ - 1)
                low_part(g + 1, 0)
            round_(NG - 1, False)
            low_part(NG - 1, NQ - 1)

        @block.scalar
        def _(act):
            for k in range(KT + 1):
                act.wait_ge(s_raw[k % 2], 16 * (k // 2 + 1) + (32 if k == KT else 0))
                n = P if k < KT else K5
                nc.scalar.activation(ws_hi[0:n, k, :], ws_raw[0:n, k % 2, :], ACT.Copy).then_inc(s_rawhi, 1)

            def high_parts(j, t):
                act.wait_ge(s_ta, t + 1)
                if not isinstance(t, int) or t >= RING:
                    act.wait_ge(s_u, (t - RING + 1) * HALVES)
                nc.scalar.activation(at_hi[:, j, 0:KT, :], ta_ps[:].rearrange("p (k b) -> p k b", k=KT),
                                     ACT.Copy).then_inc(s_athi, 1)
                nc.scalar.activation(at_hi[0:K5, j, KT, :], t5_ps[0:K5, 0:NB], ACT.Copy).then_inc(s_athi, 1)

            def split_chunk(i):
                act.wait_ge(s_chunk, (i + 1) * 16)
                nc.scalar.activation(w_hi[:, bass.ds(i * CH, CH)], chunk[:], ACT.Copy).then_inc(s_chi, 1)

            for t in range(3):
                high_parts(t % RING, t)
            split_chunk(0)
            with act.Fori(0, CHUNKS - 1) as n:
                i = n + 1
                for j in range(RING):
                    high_parts(j, i * RING + j)
                split_chunk(i)
            with act.Fori(0, T // RING - CHUNKS) as n:
                i = n + CHUNKS
                for j in range(RING):
                    high_parts(j, i * RING + j)

            act.wait_ge(s_qk, 1)
            nc.scalar.activation(qk_sb[:], pa[:, 0:D], ACT.Copy).then_inc(s_qk, 1)

            def compact(o, i):
                return nc.scalar.activation(o.rearrange("p (s t) -> p s t", t=T),
                                            i.rearrange("p (s t) -> p s t", t=TP)[:, :, 0:T], ACT.Copy)

            def act_step(g, name):
                if name == "xnT":
                    act.wait_ge(s_pe, g * 8 + 1)
                    nc.scalar.activation(xnT[:].rearrange("p a b -> p (a b)"), pa[:], ACT.Copy).then_inc(s_ac, 1)
                if name == "pT":
                    act.wait_ge(s_pe, g * 8 + 2)
                    nc.scalar.activation(pT[:].rearrange("p a b -> p (a b)"), pb[:], ACT.Copy).then_inc(s_ac, 1)
                if name == "exp":
                    act.wait_ge(s_dv, g * N_DV + DV["sub"])
                    for b in range(2):
                        v = att[b * TP:(b + 1) * TP, :, b * TP:b * TP + T]
                        nc.scalar.activation(v, v, ACT.Exp).then_inc(s_ac, 1)
                if name == "x2T":
                    act.wait_ge(s_pe, g * 8 + 6)
                    after(act, s_xlo, g)
                    compact(x2n[:], pa[:]).then_inc(s_ac, 1)
                if name == "score":
                    act.wait_ge(s_pe, g * 8 + 7)
                    nc.scalar.activation(score[0:TT, :, 0:NE],
                                         pa[0:TT, 0:PT * NE].rearrange("p (a e) -> p a e", a=PT),
                                         ACT.Copy).then_inc(s_ac, 1)
                if name == "gexp":
                    act.wait_ge(s_dv, g * N_DV + DV["gsub"])
                    nc.scalar.activation(ex[0:TT], ex[0:TT], ACT.Exp).then_inc(s_ac, 1)
                if name == "combT":
                    act.wait_ge(s_pe, g * 8 + 8)
                    after(act, s_clo2, g)
                    nc.scalar.activation(combT[:], pb[:, 0:GT], ACT.Copy).then_inc(s_ac, 1)

            def h2_copy(g):
                act.wait_ge(s_h2t, g + 1)
                after(act, s_yadd, g)
                compact(h2T[:], pb[:]).then_inc(s_h2c, 1)

            def y_copy(g):
                act.wait_ge(s_yt, g + 1)
                after(act, s_out, g * 16)
                nc.scalar.activation(y_sb[0:TT], pa[0:TT, :].rearrange("p (a o) -> p a o", a=PT),
                                     ACT.Copy).then_inc(s_yc, 1)

            def boundary(g):
                act.wait_ge(s_ac, g * 8 + AC["x2T"])
                after(act, s_x3, g * NQ)
                nc.scalar.activation(x_hi[:], x2n[:], ACT.Copy).then_inc(s_xhi, 1)
                act.wait_ge(s_ac, g * 8 + AC["combT"])
                after(act, s_cb, g * (NQ - 2))
                nc.scalar.activation(c_st[:], combT[:], ACT.Copy).then_inc(s_chi2, 1)

            def silu(g, q):
                n = g * NQ + q
                act.wait_ge(s_x1, n + 1)
                after(act, s_h, n - 1)
                nc.scalar.activation(sig[:, q % 2, :], x1_ps[:, q % 2, 0:GT], ACT.Silu).then_inc(s_silu, 1)

            def high_part(g, q):
                n = g * NQ + q
                act.wait_ge(s_h, n + 1)
                after(act, s_y, n - 1)
                nc.scalar.activation(hid_hi[:, q % 2, :], hid[:, q % 2, :], ACT.Copy).then_inc(s_hi, 1)

            def round_(g, attention):
                for q in range(2, NQ):
                    silu(g, q)
                    high_part(g, q - 1)
                    if attention:
                        for name in ("xnT", "pT", "exp", "x2T", "score", "gexp", "combT"):
                            if q == 2 + RUN[name]:
                                act_step(g + 1, name)

            for name in ("xnT", "pT", "exp", "x2T", "score", "gexp", "combT"):
                act_step(0, name)
            h2_copy(0)
            boundary(0)
            silu(0, 0)
            silu(0, 1)
            high_part(0, 0)
            with act.Fori(0, NG - 1) as g:
                round_(g, True)
                boundary(g + 1)
                high_part(g, NQ - 1)
                silu(g + 1, 0)
                silu(g + 1, 1)
                high_part(g + 1, 0)
                y_copy(g)
                h2_copy(g + 1)
            round_(NG - 1, False)
            high_part(NG - 1, NQ - 1)
            y_copy(NG - 1)

        @block.vector
        def _(dve):
            pre = [0]

            def setup(ins, wait=True):
                pre[0] += 1
                ins.then_inc(s_pre, 1)
                if wait:
                    dve.wait_ge(s_pre, pre[0])

            def vec(o):
                return steps[:, :, o - 64:o - 64 + C]

            dve.wait_ge(s_in, 48)
            setup(nc.vector.tensor_tensor(vec(O_V)[:, :, 1:C], x_sb[:, 1:, :], x_sb[:, 0:T, :], ALU.subtract), False)
            setup(nc.vector.tensor_tensor(vec(O_V)[:, :, 0], t_sb[:, 1:], t_sb[:, 0:T], ALU.subtract), False)
            setup(nc.vector.tensor_tensor(s1_sb[:, :, 1:C], x_sb[:, 0:T, :],
                                          x_sb[:, 0:1, :].to_broadcast([P, T, C - 1]), ALU.subtract), False)
            setup(nc.vector.tensor_scalar(s1_sb[:, :, 0], t_sb[:, 0:T], t_sb[:, 0:1], None, ALU.subtract), False)
            setup(nc.vector.memset(steps[:, :, O_ONE - 64], 1.0))
            setup(nc.vector.tensor_scalar(vec(O_VH), vec(O_V), 0.5, None, ALU.mult), False)
            setup(nc.vector.tensor_scalar(vec(O_VT), vec(O_V), 1.0 / 3.0, None, ALU.mult), False)
            setup(nc.vector.scalar_tensor_tensor(vec(O_E1), vec(O_V), 0.25, s1_sb[:], ALU.mult, ALU.add), False)
            setup(nc.vector.scalar_tensor_tensor(vec(O_D1), vec(O_V), 1.0 / 3.0, s1_sb[:], ALU.mult, ALU.add), False)
            setup(nc.vector.scalar_tensor_tensor(vec(O_C), vec(O_V), 0.5, s1_sb[:], ALU.mult, ALU.add))
            assert pre[0] == N_PRE
            for k in range(KT + 1):
                dve.wait_ge(s_rawhi, k + 1)
                n = P if k < KT else K5
                nc.vector.tensor_tensor(ws_lo[0:n, k, :], ws_raw[0:n, k % 2, :],
                                        ws_hi[0:n, k, :].bitcast(F32), ALU.subtract).then_inc(s_rawlo, 1)

            def outer(o, a, b, na):
                nb = b.shape[-1]
                return nc.vector.tensor_tensor(
                    o.rearrange("p (a b) -> p a b", a=na),
                    a.unsqueeze(2).to_broadcast([P, na, nb]),
                    b.unsqueeze(1).to_broadcast([P, na, nb]), ALU.mult)

            def factor(j, t):
                s = slot[:, j, :]
                dve.wait_ge(s_slot, t + 1)
                outer(small[:, 2, :], s[:, O_E1:O_E1 + C], s[:, O_VT:O_VT + C], C).then_inc(s_e, 1)
                dve.wait_ge(s_e, 3 * t + 1)
                dve.wait_ge(s_s2, t + 1)
                nc.vector.tensor_tensor(small[:, 3, :], s2r[:, j, :], small[:, 2, :], ALU.add).then_inc(s_e, 1)
                dve.wait_ge(s_e, 3 * t + 2)
                outer(e3[:], small[:, 3, :], s[:, O_VH:O_VH + C], C * C).then_inc(s_e, 1)
                dve.wait_ge(s_e, 3 * t + 3)
                dve.wait_ge(s_s3, t + 1)
                after(dve, s_ta, t)
                nc.vector.tensor_tensor(a_sb[:], s3r[:, j, :], e3[:], ALU.add).then_inc(s_a, 1)

            def low_parts(j, t):
                dve.wait_ge(s_athi, 2 * (t + 1))
                nc.vector.tensor_tensor(at_lo[:, j, 0:KT, :], ta_ps[:].rearrange("p (k b) -> p k b", k=KT),
                                        at_hi[:, j, 0:KT, :].bitcast(F32), ALU.subtract).then_inc(s_atlo, 1)
                nc.vector.tensor_tensor(at_lo[0:K5, j, KT, :], t5_ps[0:K5, 0:NB],
                                        at_hi[0:K5, j, KT, :].bitcast(F32), ALU.subtract).then_inc(s_atlo, 1)

            def tokens(i, j, t):
                after(dve, s_hst[j], 16 * i)
                for l in range(C):
                    if l % (C // HALVES) == 0:
                        dve.wait_ge(s_u, HALVES * t + l // (C // HALVES) + 1)
                    after(dve, s_acc, t * C + l)
                    prev = h_sb[:, (j - 1) % RING, :] if l == 0 else h_sb[:, j, :]
                    o = l % (C // HALVES) * D
                    nc.vector.scalar_tensor_tensor(
                        h_sb[:, j, :], u_ps[:, j, l // (C // HALVES), o:o + D],
                        slot[:, j, O_V + l:O_V + l + 1], prev, ALU.mult, ALU.add).then_inc(s_acc, 1)

            factor(0, 0)
            low_parts(0, 0)
            factor(1, 1)

            def body(i, j, t, last):
                if not last or j < RING - 1:
                    low_parts((j + 1) % RING, t + 1)
                if not last or j < RING - 2:
                    factor((j + 2) % RING, t + 2)
                tokens(i, j, t)

            steps_of_stage1(dve, body)

            dve.wait_ge(s_u, HALVES * T)
            dve.wait_ge(s_acc, C * T)
            dve.wait_ge(s_clo, CHUNKS)
            dve.wait_ge(s_s3, T + 1)
            for j in range(RING):
                dve.wait_ge(s_hst[j], 16 * (T // RING))
            nc.vector.memset(h_tok[:], 0.0)
            nc.vector.memset(att[:], 0.0)
            nc.vector.memset(mhalf[:], -0.5)
            nc.vector.memset(eps[:], EPS)
            nc.vector.memset(score[:], SENTINEL).then_inc(s_zero, 1)
            dve.wait_ge(s_zero, 1)

            def ts(o, i, a, b, op0, op1):
                return nc.vector.tensor_scalar(o, i, a, b, op0, op1)

            def norm_stats(g, src, first, base):
                for p in range(PT):
                    nc.vector.bn_stats(st[:, p, :], src[:, p, :]).then_inc(s_dv, 1)
                wait_apart(dve, s_dv, g * N_DV + base + PT, 0 if first else 1)
                for p in range(PT):
                    nc.vector.bn_aggr(mv[:, p, :], st[:, p, :]).then_inc(s_dv, 1)

            def normalise(g, src, norm):
                dve.wait_ge(s_rstd, g * 2 + norm + 1)
                for p in range(PT):
                    ts(xn[:, p, :], src[:, p, :], mv[:, p, 0:1], rstd[:, p:p + 1],
                       ALU.subtract, ALU.mult).then_inc(s_dv, 1)

            def dve_step(g, name):
                base = g * N_DV
                if name == "var1":
                    dve.wait_ge(s_load, g * 32 + 32)
                    norm_stats(g, h_tok, True, DV["var1"] - 8)
                if name == "xn1":
                    normalise(g, h_tok, 0)
                if name == "sub":
                    dve.wait_ge(s_pe, g * 8 + 4)
                    for b in range(2):
                        r = slice(b * TP, (b + 1) * TP)
                        sc = pb[r, :].rearrange("p (a q) -> p a q", a=PT)[:, :, b * TP:b * TP + T]
                        nc.vector.tensor_reduce(mx[r, :], sc, AX_X, ALU.max).then_inc(s_dv, 1)
                    for b in range(2):
                        r = slice(b * TP, (b + 1) * TP)
                        sc = pb[r, :].rearrange("p (a q) -> p a q", a=PT)[:, :, b * TP:b * TP + T]
                        dve.wait_ge(s_dv, base + DV["sub"] - 3 + b)
                        nc.vector.tensor_tensor(att[r, :, b * TP:b * TP + T], sc,
                                                mx[r, :].unsqueeze(2).to_broadcast([TP, PT, T]),
                                                ALU.subtract).then_inc(s_dv, 1)
                if name == "v":
                    dve.wait_ge(s_ac, g * 8 + AC["exp"])
                    for b in range(2):
                        r = slice(b * TP, (b + 1) * TP)
                        nc.vector.tensor_reduce(sm[r, :], att[r, :, b * TP:b * TP + T], AX_X,
                                                ALU.add).then_inc(s_dv, 1)
                    dve.wait_ge(s_dv, base + DV["v"] - 2)
                    nc.vector.reciprocal(rs[:], sm[:]).then_inc(s_dv, 1)
                    dve.wait_ge(s_dv, base + DV["v"] - 1)
                    dve.wait_ge(s_pe, g * 8 + 3)
                    nc.vector.tensor_tensor(v_sb[:], pa[:].rearrange("p (a o) -> p a o", a=PT),
                                            rs[:].unsqueeze(2).to_broadcast([P, PT, D]), ALU.mult).then_inc(s_dv, 1)
                if name == "h2":
                    dve.wait_ge(s_pe, g * 8 + 5)
                    after(dve, s_h2t, g)
                    nc.vector.tensor_tensor(h2[:], pb[:].rearrange("p (a o) -> p a o", a=PT), h_tok[:],
                                            ALU.add).then_inc(s_dv, 1)
                if name == "var2":
                    dve.wait_ge(s_dv, base + DV["h2"])
                    norm_stats(g, h2, False, DV["var2"] - 8)
                if name == "xn2":
                    normalise(g, h2, 1)
                if name == "top":
                    wait_apart(dve, s_ac, g * 8 + AC["score"], 2)
                    for p in range(PT):
                        nc.vector.max(top[0:TT, p, :], score[0:TT, p, 0:NE]).then_inc(s_dv, 1)
                if name == "gsub":
                    dve.wait_ge(s_dv, base + DV["top"])
                    nc.vector.memset(top[0:TT, :, TOPK:8], SENTINEL).then_inc(s_dv, 1)
                    nc.vector.tensor_tensor(ex[0:TT], score[0:TT, :, 0:NE],
                                            top[0:TT, :, 0:1].to_broadcast([TT, PT, NE]),
                                            ALU.subtract).then_inc(s_dv, 1)
                if name == "taken":
                    wait_apart(dve, s_dv, base + DV["gsub"] - 1, 3)
                    for p in range(PT):
                        nc.vector.match_replace(taken[0:TT, p, :], top[0:TT, p, :], score[0:TT, p, :],
                                                -SENTINEL).then_inc(s_dv, 1)
                    dve.wait_ge(s_dv, base + DV["taken"] - 1)
                    nc.vector.tensor_tensor(mask[0:TT], taken[0:TT, :, 0:NE], score[0:TT, :, 0:NE],
                                            ALU.not_equal).then_inc(s_dv, 1)
                if name == "comb":
                    dve.wait_ge(s_dv, base + DV["taken"])
                    dve.wait_ge(s_ac, g * 8 + AC["gexp"])
                    k = DV["comb"]
                    nc.vector.tensor_tensor(mask[0:TT], mask[0:TT], ex[0:TT], ALU.mult).then_inc(s_dv, 1)
                    dve.wait_ge(s_dv, base + k - 3)
                    nc.vector.tensor_reduce(gsum[0:TT], mask[0:TT], AX_X, ALU.add).then_inc(s_dv, 1)
                    dve.wait_ge(s_dv, base + k - 2)
                    nc.vector.reciprocal(grs[0:TT], gsum[0:TT]).then_inc(s_dv, 1)
                    dve.wait_ge(s_dv, base + k - 1)
                    nc.vector.tensor_tensor(
                        comb[0:TT], mask[0:TT].unsqueeze(2).to_broadcast([TT, PT, 2, NE]),
                        grs[0:TT].unsqueeze(2).unsqueeze(3).to_broadcast([TT, PT, 2, NE]),
                        ALU.mult).then_inc(s_dv, 1)

            NAMES = ("var1", "xn1", "sub", "v", "h2", "var2", "xn2", "top", "gsub", "taken", "comb")

            def boundary(g):
                dve.wait_ge(s_xhi, g + 1)
                nc.vector.tensor_tensor(x_lo[:], x2n[:], x_hi[:].bitcast(F32), ALU.subtract).then_inc(s_xlo, 1)
                dve.wait_ge(s_chi2, g + 1)
                nc.vector.tensor_tensor(c_st[NE:P, :], combT[NE:P, :], c_st[NE:P, :].bitcast(F32),
                                        ALU.subtract).then_inc(s_clo2, 1)

            def hidden(g, q):
                n = g * NQ + q
                dve.wait_ge(s_x3, n + 1)
                dve.wait_ge(s_silu, n + 1)
                x3 = x3_ps[:, q % 2, 0:GT]
                if q < 2:
                    after(dve, s_lo, n - 1)
                    nc.vector.tensor_tensor(hid[:, q % 2, :], x3, sig[:, q % 2, :], ALU.mult).then_inc(s_h, 1)
                else:
                    m = g * (NQ - 2) + q - 2
                    nc.vector.tensor_tensor(gat[:, q % 2, :], x3, sig[:, q % 2, :], ALU.mult).then_inc(s_g, 1)
                    dve.wait_ge(s_cb, m + 1)
                    after(dve, s_lo, n - 1)
                    dve.wait_ge(s_g, m + 1)
                    nc.vector.tensor_tensor(hid[:, q % 2, :], cb_ps[:, 0:GT], gat[:, q % 2, :],
                                            ALU.mult).then_inc(s_h, 1)

            def finish(g):
                dve.wait_ge(s_y, g * NQ + NQ)
                dve.wait_ge(s_h2c, g + 1)
                after(dve, s_yt, g)
                nc.vector.tensor_tensor(yT[:], y_ps[:, 0:GT], h2T[:], ALU.add).then_inc(s_yadd, 1)

            def round_(g, attention):
                for q in range(2, NQ):
                    hidden(g, q)
                    if attention:
                        for name in NAMES:
                            if q == 2 + RUN[name]:
                                dve_step(g + 1, name)

            for name in NAMES:
                dve_step(0, name)
            boundary(0)
            hidden(0, 0)
            hidden(0, 1)
            with dve.Fori(0, NG - 1) as g:
                round_(g, True)
                boundary(g + 1)
                hidden(g + 1, 0)
                finish(g)
                hidden(g + 1, 1)
            round_(NG - 1, False)
            finish(NG - 1)

        @block.tensor
        def _(pe):
            def three(o, lhs_hi, lhs_lo, rhs_hi, rhs_lo, first=True, last=True):
                nc.tensor.matmul(o, lhs_hi, rhs_hi, start=first, stop=False)
                nc.tensor.matmul(o, lhs_lo, rhs_hi, start=False, stop=False)
                return nc.tensor.matmul(o, lhs_hi, rhs_lo, start=False, stop=last)

            def transposes(j, t):
                pe.wait_ge(s_a, t + 1)
                pe.wait_ge(s_b, t + 1)
                after(pe, s_atlo, 2 * t)
                for k in range(KT):
                    nc.tensor.transpose(ta_ps[:, k * P:(k + 1) * P], a_sb[:, k * P:(k + 1) * P], ident[:])
                nc.tensor.transpose(t5_ps[0:K5, 0:NB], slot[:, j, 0:K5], ident[:]).then_inc(s_ta, 1)

            def project(j, t, first=False):
                pe.wait_ge(s_atlo, 2 * (t + 1))
                if not isinstance(t, int) or t >= RING:
                    pe.wait_ge(s_acc, (t - RING + 1) * C)
                for h in range(HALVES):
                    cols = slice(h * (NU // HALVES), (h + 1) * (NU // HALVES))
                    for k in range(KT + 1):
                        if first and h == 0:
                            pe.wait_ge(s_rawlo, k + 1)
                        n = P if k < KT else K5
                        mm = three(u_ps[:, j, h, :], at_hi[0:n, j, k, :], at_lo[0:n, j, k, :],
                                   ws_hi[0:n, k, cols], ws_lo[0:n, k, cols], k == 0, k == KT)
                    mm.then_inc(s_u, 1)

            pe.wait_ge(s_id, 2)
            transposes(0, 0)
            for t in range(RING):
                transposes((t + 1) % RING, t + 1)
                project(t, t, t == 0)
            with pe.Fori(0, T // RING - 2) as n:
                i = n + 1
                for j in range(RING):
                    transposes((j + 1) % RING, i * RING + j + 1)
                    project(j, i * RING + j)
            for t in range(T - RING, T):
                if t + 1 < T:
                    transposes((t + 1) % RING, t + 1)
                project(t % RING, t)

            pe.wait_ge(s_wqk, 64)
            pe.wait_ge(s_acc, C * T)
            nc.tensor.matmul(pa[:, 0:D], wq_sb[:], wk_sb[:], start=True, stop=True).then_inc(s_qk, 1)
            pe.wait_ge(s_qk, 2)

            def group(g, o, pairs):
                for p in range(PT):
                    lhs, rhs = pairs(p)
                    mm = nc.tensor.matmul(o[:, p, :], lhs, rhs, start=True, stop=True)
                return mm.then_inc(s_pe, 1)

            def transpose_group(src, bank):
                for p in range(PT):
                    mm = nc.tensor.transpose(bank[:, p * P:(p + 1) * P], src[:, p, :], ident[:])
                return mm

            pa3 = pa[:].rearrange("p (a q) -> p a q", a=PT)
            pb3 = pb[:].rearrange("p (a q) -> p a q", a=PT)

            def pe_step(g, name):
                base = g * N_DV
                if name == "pe_xnT":
                    pe.wait_ge(s_dv, base + DV["xn1"])
                    after(pe, s_yc, g - 1) if not isinstance(g, int) or g > 1 else None
                    transpose_group(xn, pa).then_inc(s_pe, 1)
                if name == "pe_pT":
                    pe.wait_ge(s_ac, g * 8 + AC["xnT"])
                    after(pe, s_h2c, g)
                    nc.tensor.matmul(pb[:], qk_sb[:], xnT[:].rearrange("p a b -> p (a b)"), start=True,
                                     stop=True).then_inc(s_pe, 1)
                    group(g, pa3, lambda p: (xnT[:, p, :], wv_sb[:]))
                if name == "pe_score":
                    pe.wait_ge(s_ac, g * 8 + AC["pT"])
                    group(g, pb3, lambda p: (xnT[:, p, :], pT[:, p, :]))
                if name == "pe_out":
                    pe.wait_ge(s_dv, base + DV["v"])
                    group(g, pb3, lambda p: (att[:, p, :], v_sb[:, p, :]))
                if name == "pe_x2T":
                    pe.wait_ge(s_dv, base + DV["xn2"])
                    transpose_group(xn, pa).then_inc(s_pe, 1)
                if name == "pe_gate":
                    pe.wait_ge(s_ac, g * 8 + AC["x2T"])
                    for p in range(PT):
                        mm = nc.tensor.matmul(pa[0:TT, p * NE:(p + 1) * NE], x2n[:, p * TT:(p + 1) * TT],
                                              wg_sb[:], start=True, stop=True)
                    mm.then_inc(s_pe, 1)
                if name == "pe_combT":
                    pe.wait_ge(s_dv, base + DV["comb"])
                    for p in range(PT):
                        mm = nc.tensor.transpose(pb[:, p * TT:(p + 1) * TT],
                                                 comb[0:TT, p].rearrange("p a e -> p (a e)"), ident[0:TT, 0:TT])
                    mm.then_inc(s_pe, 1)

            NAMES = ("pe_xnT", "pe_pT", "pe_score", "pe_out", "pe_x2T", "pe_gate", "pe_combT")

            def w(kind, q, part):
                c = (kind * NQ + q) * P
                return part[:, c:c + P]

            def up(g, q):
                n = g * NQ + q
                if q == 0:
                    pe.wait_ge(s_xhi, g + 1)
                after(pe, s_silu, n - 1)
                nc.tensor.matmul(x1_ps[:, q % 2, 0:GT], w(0, q, w_lo), x_hi[:], start=True, stop=False)
                nc.tensor.matmul(x1_ps[:, q % 2, 0:GT], w(0, q, w_hi), x_hi[:], start=False, stop=False)
                if q == 0:
                    pe.wait_ge(s_xlo, g + 1)
                nc.tensor.matmul(x1_ps[:, q % 2, 0:GT], w(0, q, w_hi), x_lo[:], start=False,
                                 stop=True).then_inc(s_x1, 1)
                after(pe, s_h, n - 1)
                three(x3_ps[:, q % 2, 0:GT], w(1, q, w_hi), w(1, q, w_lo), x_hi[:], x_lo[:]).then_inc(s_x3, 1)
                if q >= 2:
                    if q == 2:
                        pe.wait_ge(s_exp, 1)
                        pe.wait_ge(s_clo2, g + 1)
                    pe.wait_ge(s_h, n)
                    e = 2 * (q - 2)
                    nc.tensor.matmul(cb_ps[:, 0:GT], expand[:, e:e + 2, :].rearrange("p e i -> p (e i)"), c_st[:], start=True, stop=True).then_inc(s_cb, 1)

            def down(g, q):
                n = g * NQ + q
                pe.wait_ge(s_hi, n + 1)
                pe.wait_ge(s_lo, n + 1)
                if q == 0:
                    after(pe, s_yadd, g)
                three(y_ps[:, 0:GT], w(2, q, w_hi), w(2, q, w_lo), hid_hi[:, q % 2, :], hid_lo[:, q % 2, :],
                      q == 0, q == NQ - 1).then_inc(s_y, 1)

            def y_transpose(g):
                pe.wait_ge(s_yadd, g + 1)
                pe.wait_ge(s_ac, g * 8 + 8 + AC["score"]) if not isinstance(g, int) or g < NG - 1 else None
                for p in range(PT):
                    mm = nc.tensor.transpose(pa[0:TT, p * D:(p + 1) * D], yT[:, p * TT:(p + 1) * TT], ident[:])
                mm.then_inc(s_yt, 1)

            def h2_transpose(g):
                pe.wait_ge(s_ac, g * 8 + AC["combT"])
                transpose_group(h2, pb).then_inc(s_h2t, 1)

            def round_(g, attention):
                for q in range(2, NQ):
                    up(g, q)
                    down(g, q - 2)
                    if attention:
                        for name in NAMES:
                            if q == 2 + RUN[name]:
                                pe_step(g + 1, name)

            for name in NAMES:
                pe_step(0, name)
            h2_transpose(0)
            pe.wait_ge(s_clo, CHUNKS)
            up(0, 0)
            up(0, 1)
            with pe.Fori(0, NG - 1) as g:
                round_(g, True)
                down(g, NQ - 2)
                up(g + 1, 0)
                down(g, NQ - 1)
                up(g + 1, 1)
                y_transpose(g)
                h2_transpose(g + 1)
            round_(NG - 1, False)
            down(NG - 1, NQ - 2)
            down(NG - 1, NQ - 1)
            y_transpose(NG - 1)


N_PRE = 10
DV = {}
_n = 0
for _name, _ops in (("var1", 8), ("xn1", 4), ("sub", 4), ("v", 4), ("h2", 1), ("var2", 8), ("xn2", 4),
                    ("top", 4), ("gsub", 2), ("taken", 5), ("comb", 4)):
    _n += _ops
    DV[_name] = _n
N_DV = _n
AC = {"xnT": 1, "pT": 2, "exp": 4, "x2T": 5, "score": 6, "gexp": 7, "combT": 8}
RUN = {"var1": 0, "rstd1": 2, "xn1": 2, "pe_xnT": 4, "xnT": 4, "pe_pT": 6, "pT": 6, "pe_score": 7, "sub": 8,
       "exp": 9, "v": 10, "pe_out": 12, "h2": 12, "var2": 13, "rstd2": 15, "xn2": 15, "pe_x2T": 17, "x2T": 17,
       "pe_gate": 18, "score": 18, "top": 19, "gsub": 20, "taken": 21, "gexp": 21, "comb": 23, "pe_combT": 25,
       "combT": 25}


def kernel(x, L0_tok_W, L0_tok_b, L0_attn_Wq, L0_attn_Wk, L0_attn_Wv, L0_ffn_w_gate, L0_ffn_w1, L0_ffn_w2,
           L0_ffn_w3, L0_ffn_w_sg, L0_ffn_w_su, L0_ffn_w_sd):
    import numpy as np
    import concourse.bacc as bacc
    from concourse.bass_utils import run_bass_kernel_spmd

    ffw = np.concatenate([
        np.transpose(L0_ffn_w_sg), np.transpose(L0_ffn_w1, (2, 0, 1)).reshape(D, -1),
        np.transpose(L0_ffn_w_su), np.transpose(L0_ffn_w3, (2, 0, 1)).reshape(D, -1),
        np.transpose(np.concatenate([np.transpose(L0_ffn_w_sd), np.asarray(L0_ffn_w2).reshape(-1, D)])
                     .reshape(NQ, P, D), (1, 0, 2)).reshape(P, -1)], axis=1)
    arrays = {
        "x": np.asarray(x).reshape(NB, -1),
        "tgrid": np.linspace(0.0, 1.0, T + 1, dtype=np.float32).reshape(1, -1),
        "wt": np.transpose(L0_tok_W), "bias": np.asarray(L0_tok_b).reshape(1, -1),
        "wq": L0_attn_Wq, "wk": L0_attn_Wk, "wvt": np.transpose(L0_attn_Wv),
        "wgt": np.transpose(L0_ffn_w_gate), "ffw": ffw}
    arrays = {k: np.ascontiguousarray(a) for k, a in arrays.items()}
    nc = bacc.Bacc("TRN2", target_bir_lowering=False, num_devices=1)
    args = [nc.dram_tensor(k, a.shape, mybir.dt.from_np(a.dtype), kind="ExternalInput").ap()
            for k, a in arrays.items()]
    out = nc.dram_tensor("out", (NB * T, D), F32, kind="ExternalOutput").ap()
    audio_tower(nc, *args, out)
    r = run_bass_kernel_spmd(nc, [arrays], core_ids=[0])
    return r.results[0]["out"].reshape(NB, T, D)
```

```python
from contextlib import ExitStack

import concourse.bass as bass
from concourse import mybir

F32 = mybir.dt.float32
F32R = mybir.dt.float32r
ALU = mybir.AluOpType
ACT = mybir.ActivationFunctionType
AX_X = mybir.AxisListType.X

P = 128
NB = 128
T = 63
C = 8
D = 128
NE = 64
TOPK = 6
KT = C ** 3 // P
K5 = C * C + C + 1
NU = C * D
RING = 3
HALVES = 2
GB = 8
NG = NB // GB
PT = GB // 2
TP = 64
GT = GB * T
TT = 2 * T
NQ = 2 + NE // 2
LAG = 4
BATCH = 4
NBATCH = (NQ - 2) // BATCH
HEAD = 7
WCOLS = 3 * NQ * P
CHUNKS = 16
CH = WCOLS // CHUNKS
EPS = 1e-5
SENTINEL = 3.0e38
O_C, O_ONE, O_V, O_VH, O_VT, O_E1, O_D1 = 64, 72, 73, 81, 89, 97, 105
SLOT = 113
PK = SLOT - 64
N_DV = 47


def audio_tower(nc, x, tgrid, wt, bias, wq, wk, wvt, wgt, ffw, out):
    h_dram = nc.dram_tensor("h_tokens", (NB, T, D), F32).ap()
    comb_dram = nc.dram_tensor("routing_weights", (NG, NE, GT), F32).ap()
    comb_store = comb_dram.rearrange("g e (a h t) -> g h e a t", h=2, t=TT)
    h_load = h_dram.rearrange("(g p b) t o -> g b t p o", p=PT, b=2)
    out_rows = out.rearrange("(g p b t) o -> g b t p o", p=PT, b=2, t=T)

    with ExitStack() as ctx:
        def sem(name):
            return ctx.enter_context(nc.semaphore(name))

        def sb(name, shape, dt=F32, scope=ctx):
            return scope.enter_context(nc.sbuf_tensor(name, shape, dt))

        ident = sb("ident", [P, P])
        w_hi = sb("w_hi", [P, WCOLS], F32R)
        w_lo = sb("w_lo", [P, WCOLS], F32R)
        wq_sb = sb("wq_sb", [P, D])
        wk_sb = sb("wk_sb", [P, D])
        wv_sb = sb("wv_sb", [P, D])
        wg_sb = sb("wg_sb", [P, NE])
        qk_sb = sb("qk_sb", [P, D])
        s1 = ExitStack()
        p1 = ExitStack()
        ws_hi = sb("ws_hi", [P, KT + 1, NU], F32R, s1)
        ws_lo = sb("ws_lo", [P, KT + 1, NU], F32R, s1)
        ws_raw = sb("ws_raw", [P, 2, NU], F32, s1)
        x_sb = sb("x_sb", [P, T + 1, C - 1], F32, s1)
        t_sb = sb("t_sb", [P, T + 1], F32, s1)
        s1_sb = sb("s1_sb", [P, T, C], F32, s1)
        steps = sb("steps", [P, T, PK], F32, s1)
        slot = sb("slot", [P, RING, SLOT], F32, s1)
        s2r = sb("s2r", [P, RING, C * C], F32, s1)
        s3r = sb("s3r", [P, RING, C ** 3], F32, s1)
        small = sb("small", [P, 4, C * C], F32, s1)
        b3 = sb("b3", [P, C ** 3], F32, s1)
        e3 = sb("e3", [P, C ** 3], F32, s1)
        a_sb = sb("a_sb", [P, C ** 3], F32, s1)
        at_hi = sb("at_hi", [P, RING, KT + 1, NB], F32R, s1)
        at_lo = sb("at_lo", [P, RING, KT + 1, NB], F32R, s1)
        h_sb = sb("h_sb", [P, RING, D], F32, s1)
        chunk = sb("chunk", [P, CH], F32, s1)
        u_ps = p1.enter_context(nc.psum_tensor("u_ps", [P, RING, HALVES, NU // HALVES], F32))
        ta_ps = p1.enter_context(nc.psum_tensor("ta_ps", [P, C ** 3], F32))
        t5_ps = p1.enter_context(nc.psum_tensor("t5_ps", [P, 512], F32))
        s1.close()
        p1.close()
        h_tok = sb("h_tok", [P, PT, D])
        st = sb("st", [P, PT, 6])
        mv = sb("mv", [P, PT, 2])
        vare = sb("vare", [P, PT])
        rstd = sb("rstd", [P, PT])
        mhalf = sb("mhalf", [P, PT])
        eps = sb("eps", [P, PT])
        xn = sb("xn", [P, PT, D])
        xnT = sb("xnT", [P, PT, P])
        pT = sb("pT", [P, PT, P])
        att = sb("att", [P, PT, P])
        mx = sb("mx", [P, PT])
        sm = sb("sm", [P, PT])
        rs = sb("rs", [P, PT])
        v_sb = sb("v_sb", [P, PT, D])
        h2 = sb("h2", [P, PT, D])
        x2n = sb("x2n", [P, GT])
        h2_kept = sb("h2_kept", [P, PT, D])
        combT = sb("combT", [P, PT // 2, TT])
        score = sb("score", [P, PT, NE + 2])
        taken = sb("taken", [P, PT, NE + 2])
        top = sb("top", [P, PT, 8])
        ex = sb("ex", [P, PT, NE])
        mask = sb("mask", [P, PT, NE])
        spare = sb("spare", [P, 4])
        gsum = sb("gsum", [P, PT])
        grs = sb("grs", [P, PT])
        comb = sb("comb", [P, PT, NE])
        x_hi = sb("x_hi", [P, GT], F32R)
        x_lo = sb("x_lo", [P, GT], F32R)
        cbb = sb("cbb", [P, 2, BATCH, GT])
        sig = sb("sig", [P, 2, GT])
        scaled = sb("scaled", [P, 2, GT])
        hid = sb("hid", [P, HID_SLOTS, GT])
        hid_hi = sb("hid_hi", [P, HID_SLOTS, GT], F32R)
        hid_lo = sb("hid_lo", [P, HID_SLOTS, GT], F32R)
        yT = sb("yT", [P, PT, 2, TP])
        y_sb = sb("y_sb", [P, PT, D])
        x1_ps = ctx.enter_context(nc.psum_tensor("x1_ps", [P, 2, 512], F32))
        x3_ps = ctx.enter_context(nc.psum_tensor("x3_ps", [P, 3, 512], F32))
        y_ps = ctx.enter_context(nc.psum_tensor("y_ps", [P, 512], F32))
        pa = ctx.enter_context(nc.psum_tensor("pa", [P, 512], F32))
        pb = ctx.enter_context(nc.psum_tensor("pb", [P, 512], F32))

        s_in = sem("s_in")
        s_wqk = sem("s_wqk")
        s_raw = [sem("s_raw0"), sem("s_raw1")]
        s_rawhi = sem("s_rawhi")
        s_rawlo = sem("s_rawlo")
        s_chunk = sem("s_chunk")
        s_chi = sem("s_chi")
        s_clo = sem("s_clo")
        s_id = sem("s_id")
        s_pre = sem("s_pre")
        s_slot = sem("s_slot")
        s_pool = sem("s_pool")
        s_b = sem("s_b")
        s_s2 = sem("s_s2")
        s_s3 = sem("s_s3")
        s_e = sem("s_e")
        s_a = sem("s_a")
        s_ta = sem("s_ta")
        s_athi = sem("s_athi")
        s_atlo = sem("s_atlo")
        s_u = sem("s_u")
        s_acc = sem("s_acc")
        s_hst = [sem(f"s_hst{j}") for j in range(RING)]
        s_load = sem("s_load")
        s_dv = sem("s_dv")
        s_rstd = sem("s_rstd")
        s_veps = sem("s_veps")
        s_pe = sem("s_pe")
        s_ac = sem("s_ac")
        s_zero = sem("s_zero")
        s_qk = sem("s_qk")
        s_xhi = sem("s_xhi")
        s_xlo = sem("s_xlo")
        s_comb = sem("s_comb")
        s_cbb = [sem("s_cbb0"), sem("s_cbb1")]
        s_x1 = sem("s_x1")
        s_x3 = sem("s_x3")
        s_y = sem("s_y")
        s_silu = sem("s_silu")
        s_sc = sem("s_sc")
        s_h = sem("s_h")
        s_hi = sem("s_hi")
        s_lo = sem("s_lo")
        s_yc = sem("s_yc")
        s_yt = sem("s_yt")
        s_fin = sem("s_fin")
        s_kept = sem("s_kept")
        s_out = sem("s_out")

        def after(eng, s, value):
            if not isinstance(value, int) or value > 0:
                eng.wait_ge(s, value)

        def last_use(slots, g, q):
            d = 1
            while slots[(q - d) % NQ] != slots[q]:
                d += 1
            return g * NQ + q - d + 1

        def wait_apart(eng, s, value, place):
            eng.wait_ge(s, value)
            nc.vector.memset(spare[:, place:place + 1], 0.0)

        block = ctx.enter_context(nc.Block())

        @block.sync
        def _(sp):
            sp.dma_start(x_sb[:].rearrange("p t c -> p (t c)"), x).then_inc(s_in, 16)
            sp.dma_start(t_sb[:], tgrid.to_broadcast([P, T + 1])).then_inc(s_in, 16)
            sp.dma_start(h_sb[:, RING - 1, :], bias.to_broadcast([P, D])).then_inc(s_in, 16)
            w4 = wt[C + C * C + C ** 3:, :].rearrange("(k p l) o -> k p (l o)", k=KT, l=C)
            for k in range(KT + 1):
                if k >= 2:
                    sp.wait_ge(s_rawlo, k - 1)
                if k < KT:
                    sp.dma_start(ws_raw[:, k % 2, :], w4[k]).then_inc(s_raw[k % 2], 16)
                else:
                    for r0, n, w0 in ((0, C * C, C + C * C), (C * C, C, C), (C * C + C, 1, 0)):
                        sp.dma_start(
                            ws_raw[r0:r0 + n, k % 2, :],
                            wt[w0:w0 + n * C, :].rearrange("(p l) o -> p (l o)", l=C),
                        ).then_inc(s_raw[k % 2], 16)
            sp.dma_start(wq_sb[:], wq).then_inc(s_wqk, 16)
            sp.dma_start(wk_sb[:], wk).then_inc(s_wqk, 16)
            sp.dma_start(wv_sb[:], wvt).then_inc(s_wqk, 16)
            sp.dma_start(wg_sb[:], wgt).then_inc(s_wqk, 16)

            def load_chunk(i):
                after(sp, s_clo, i)
                sp.dma_start(chunk[:], ffw[:, bass.ds(i * CH, CH)]).then_inc(s_chunk, 16)

            def store_h(i, j, t, last):
                sp.wait_ge(s_acc, (t + 1) * C)
                sp.dma_start(h_dram[:, t, :], h_sb[:, j, :]).then_inc(s_hst[j], 16)

            load_chunk(0)
            with sp.Fori(0, CHUNKS - 1) as i:
                for j in range(RING):
                    store_h(i, j, i * RING + j, False)
                load_chunk(i + 1)
            with sp.Fori(0, T // RING - CHUNKS + 1) as n:
                i = n + CHUNKS - 1
                for j in range(RING):
                    store_h(i, j, i * RING + j, False)

            def load_group(g):
                for b in range(2):
                    sp.dma_start(h_tok[b * TP:b * TP + T, :, :], h_load[g, b]).then_inc(s_load, 16)

            def store_group(g):
                sp.wait_ge(s_fin, g + 2)
                for b in range(2):
                    sp.dma_start(out_rows[g, b], y_sb[b * TP:b * TP + T, :, :]).then_inc(s_out, 16)

            for j in range(RING):
                sp.wait_ge(s_hst[j], 16 * (T // RING))
            sp.wait_ge(s_zero, 1)
            load_group(0)
            sp.wait_ge(s_dv, DV["h2"])
            load_group(1)

            def store_comb(g):
                sp.wait_ge(s_ac, g * 8 + AC["combT"])
                for h in range(2):
                    sp.dma_start(comb_store[g, h], combT[h * NE:(h + 1) * NE, :, :]).then_inc(s_comb, 16)

            def load_batch(g, k, wait=True):
                if k == 0:
                    sp.wait_ge(s_comb, (g + 1) * 32)
                if wait:
                    sp.wait_ge(s_sc, g * (NQ - 2) + (k - 1) * BATCH)
                e = 2 * BATCH * k
                for b in range(2):
                    rows = comb_dram[g, e + b:e + 2 * BATCH:2, :]
                    sp.dma_start(cbb[b * NE:(b + 1) * NE, k % 2, :, :],
                                 rows.unsqueeze(0).to_broadcast([NE, BATCH, GT])).then_inc(s_cbb[k % 2], 16)

            def first_batches(g, wait):
                store_comb(g)
                load_batch(g, 0, wait)
                load_batch(g, 1, wait)
                load_batch(g, 2)

            first_batches(0, False)
            with sp.Fori(0, NG - 2) as g:
                for k in range(3, NBATCH):
                    load_batch(g, k)
                    if k == 5:
                        sp.wait_ge(s_dv, (g + 1) * N_DV + DV["h2"])
                        load_group(g + 2)
                first_batches(g + 1, True)
                store_group(g)
            for g in range(NG - 2, NG):
                for k in range(3, NBATCH):
                    load_batch(g, k)
                if g + 1 < NG:
                    first_batches(g + 1, True)
                store_group(g)
            sp.wait_ge(s_out, 32 * NG + 1)

        @block.gpsimd
        def _(pool):
            nc.gpsimd.memset(ident[:], 0.0).then_inc(s_id, 1)
            pool.wait_ge(s_id, 1)
            nc.gpsimd.affine_select(out=ident[:], in_=ident[:], compare_op=ALU.not_equal, fill=1.0, base=0,
                                    pattern=[[-1, P]], channel_multiplier=1).then_inc(s_id, 1)
            nc.gpsimd.memset(s2r[:, 0, :], 0.0).then_inc(s_s2, 1)
            nc.gpsimd.memset(s3r[:, 0, :], 0.0).then_inc(s_s3, 1)
            pool.wait_ge(s_pre, N_PRE)

            def outer(o, a, b, na):
                nb = b.shape[-1]
                return nc.gpsimd.tensor_tensor(
                    o.rearrange("p (a b) -> p a b", a=na),
                    a.unsqueeze(2).to_broadcast([P, na, nb]),
                    b.unsqueeze(1).to_broadcast([P, na, nb]), ALU.mult)

            def state(i, j, t, last):
                nx = (j + 1) % RING
                s = slot[:, j, :]
                after(pool, s_acc, (t - RING + 1) * C if not isinstance(t, int) or t >= RING else 0)
                nc.gpsimd.tensor_copy(s[:, 64:SLOT], steps[:, t, :]).then_inc(s_slot, 1)
                pool.wait_ge(s_slot, t + 1)
                outer(small[:, 0, :], s[:, O_D1:O_D1 + C], s[:, O_VH:O_VH + C], C).then_inc(s_pool, 1)
                outer(small[:, 1, :], s[:, O_C:O_C + C], s[:, O_V:O_V + C], C).then_inc(s_pool, 1)
                pool.wait_ge(s_pool, 3 * t + 1)
                pool.wait_ge(s_s2, t + 1)
                nc.gpsimd.tensor_tensor(s[:, 0:64], s2r[:, j, :], small[:, 0, :], ALU.add).then_inc(s_b, 1)
                pool.wait_ge(s_pool, 3 * t + 2)
                pool.wait_ge(s_a, t - 1) if not isinstance(t, int) or t > 1 else None
                nc.gpsimd.tensor_tensor(s2r[:, nx, :], s2r[:, j, :], small[:, 1, :], ALU.add).then_inc(s_s2, 1)
                pool.wait_ge(s_b, t + 1)
                outer(b3[:], s[:, 0:64], s[:, O_V:O_V + C], C * C).then_inc(s_pool, 1)
                pool.wait_ge(s_pool, 3 * t + 3)
                pool.wait_ge(s_s3, t + 1)
                nc.gpsimd.tensor_tensor(s3r[:, nx, :], s3r[:, j, :], b3[:], ALU.add).then_inc(s_s3, 1)

            def split_chunk(i):
                pool.wait_ge(s_chi, i + 1)
                nc.gpsimd.tensor_tensor(w_lo[:, bass.ds(i * CH, CH)], chunk[:],
                                        w_hi[:, bass.ds(i * CH, CH)].bitcast(F32), ALU.subtract).then_inc(s_clo, 1)

            for t in range(2):
                state(0, t, t, False)
            state(0, 2, 2, False)
            split_chunk(0)
            with pool.Fori(0, CHUNKS - 1) as n:
                i = n + 1
                for j in range(RING):
                    state(i, j, i * RING + j, False)
                split_chunk(i)
            with pool.Fori(0, T // RING - CHUNKS) as n:
                i = n + CHUNKS
                for j in range(RING):
                    state(i, j, i * RING + j, False)

            pool.wait_ge(s_zero, 1)

            def inverse_std(g, norm):
                pool.wait_ge(s_dv, g * N_DV + DV["var1" if norm == 0 else "var2"])
                nc.gpsimd.tensor_tensor(vare[:], mv[:, :, 1], eps[:], ALU.add).then_inc(s_veps, 1)
                pool.wait_ge(s_veps, g * 2 + norm + 1)
                nc.gpsimd.tensor_tensor(rstd[:], vare[:], mhalf[:], ALU.pow).then_inc(s_rstd, 1)

            def scale(g, q):
                n = g * NQ + q
                k = (q - 2) // BATCH
                pool.wait_ge(s_silu, n + 1)
                pool.wait_ge(s_cbb[k % 2], 32 * (g * (NBATCH // 2) + k // 2 + 1))
                after(pool, s_h, n - 1)
                nc.gpsimd.tensor_tensor(scaled[:, q % 2, :], sig[:, q % 2, :], cbb[:, k % 2, (q - 2) % BATCH, :],
                                        ALU.mult).then_inc(s_sc, 1)

            def pairs(g, qs, attention=False, prev=True):
                for q in qs:
                    if q >= 2:
                        scale(g, q)
                    if attention and q == RUN["rstd1"]:
                        inverse_std(g + 1, 0)
                    if attention and q == RUN["rstd2"]:
                        inverse_std(g + 1, 1)

            inverse_std(0, 0)
            inverse_std(0, 1)
            pairs(0, range(HEAD), prev=False)
            with pool.Fori(0, NG - 1) as g:
                pairs(g, range(HEAD, NQ), attention=True)
                pairs(g + 1, range(HEAD))
            pairs(NG - 1, range(HEAD, NQ))

        @block.scalar
        def _(act):
            for k in range(KT + 1):
                act.wait_ge(s_raw[k % 2], 16 * (k // 2 + 1) + (32 if k == KT else 0))
                n = P if k < KT else K5
                nc.scalar.activation(ws_hi[0:n, k, :], ws_raw[0:n, k % 2, :], ACT.Copy).then_inc(s_rawhi, 1)

            def high_parts(j, t):
                act.wait_ge(s_ta, t + 1)
                if not isinstance(t, int) or t >= RING:
                    act.wait_ge(s_u, (t - RING + 1) * HALVES)
                nc.scalar.activation(at_hi[:, j, 0:KT, :], ta_ps[:].rearrange("p (k b) -> p k b", k=KT),
                                     ACT.Copy).then_inc(s_athi, 1)
                nc.scalar.activation(at_hi[0:K5, j, KT, :], t5_ps[0:K5, 0:NB], ACT.Copy).then_inc(s_athi, 1)

            def split_chunk(i):
                act.wait_ge(s_chunk, (i + 1) * 16)
                nc.scalar.activation(w_hi[:, bass.ds(i * CH, CH)], chunk[:], ACT.Copy).then_inc(s_chi, 1)

            for t in range(3):
                high_parts(t % RING, t)
            split_chunk(0)
            with act.Fori(0, CHUNKS - 1) as n:
                i = n + 1
                for j in range(RING):
                    high_parts(j, i * RING + j)
                split_chunk(i)
            with act.Fori(0, T // RING - CHUNKS) as n:
                i = n + CHUNKS
                for j in range(RING):
                    high_parts(j, i * RING + j)

            act.wait_ge(s_qk, 1)
            nc.scalar.activation(qk_sb[:], pa[:, 0:D], ACT.Copy).then_inc(s_qk, 1)

            def compact(o, i):
                return nc.scalar.activation(o.rearrange("p (s t) -> p s t", t=T),
                                            i.rearrange("p (s t) -> p s t", t=TP)[:, :, 0:T], ACT.Copy)

            def act_step(g, name):
                if name == "xnT":
                    act.wait_ge(s_pe, g * 8 + 1)
                    nc.scalar.activation(xnT[:].rearrange("p a b -> p (a b)"), pa[:], ACT.Copy).then_inc(s_ac, 1)
                if name == "pT":
                    act.wait_ge(s_pe, g * 8 + 2)
                    nc.scalar.activation(pT[:].rearrange("p a b -> p (a b)"), pb[:], ACT.Copy).then_inc(s_ac, 1)
                if name == "exp":
                    act.wait_ge(s_dv, g * N_DV + DV["sub"])
                    for b in range(2):
                        v = att[b * TP:(b + 1) * TP, :, b * TP:b * TP + T]
                        nc.scalar.activation(v, v, ACT.Exp).then_inc(s_ac, 1)
                if name == "x2T":
                    act.wait_ge(s_pe, g * 8 + 6)
                    after(act, s_xlo, g)
                    compact(x2n[:], pa[:]).then_inc(s_ac, 1)
                if name == "score":
                    act.wait_ge(s_pe, g * 8 + 7)
                    nc.scalar.activation(score[0:TT, :, 0:NE],
                                         pa[0:TT, 0:PT * NE].rearrange("p (a e) -> p a e", a=PT),
                                         ACT.Copy).then_inc(s_ac, 1)
                if name == "gexp":
                    act.wait_ge(s_dv, g * N_DV + DV["gsub"])
                    nc.scalar.activation(ex[0:TT], ex[0:TT], ACT.Exp).then_inc(s_ac, 1)
                if name == "combT":
                    act.wait_ge(s_pe, g * 8 + 8)
                    after(act, s_comb, 32 * g)
                    nc.scalar.activation(combT[:].rearrange("p a t -> p (a t)"), pb[:, 0:GT // 2], ACT.Copy).then_inc(s_ac, 1)

            def y_copy(g):
                act.wait_ge(s_y, (g + 1) * NQ)
                act.wait_ge(s_fin, g + 1)
                nc.scalar.activation(yT[:].rearrange("p a b t -> p (a b) t")[:, :, 0:T],
                                     y_ps[:, 0:GT].rearrange("p (s t) -> p s t", t=T), ACT.Copy).then_inc(s_yc, 1)

            def keep(g):
                act.wait_ge(s_fin, g + 1)
                act.wait_ge(s_dv, g * N_DV + DV["h2"])
                nc.scalar.activation(h2_kept[:], h2[:], ACT.Copy).then_inc(s_kept, 1)

            def x_high(g):
                act.wait_ge(s_ac, g * 8 + AC["x2T"])
                after(act, s_x3, g * NQ)
                nc.scalar.activation(x_hi[:], x2n[:], ACT.Copy).then_inc(s_xhi, 1)

            def silu(g, q):
                n = g * NQ + q
                act.wait_ge(s_x1, n + 1)
                if q in (2, 3):
                    after(act, s_h, n - 1)
                else:
                    after(act, s_sc, g * (NQ - 2) + q - (1 if q < 2 else 3))
                nc.scalar.activation(sig[:, q % 2, :], x1_ps[:, q % 2, 0:GT], ACT.Silu).then_inc(s_silu, 1)

            def high_part(g, q):
                act.wait_ge(s_h, g * NQ + q + 1)
                after(act, s_y, last_use(HID_SLOT, g, q))
                k = HID_SLOT[q]
                nc.scalar.activation(hid_hi[:, k, :], hid[:, k, :], ACT.Copy).then_inc(s_hi, 1)

            NAMES = ("xnT", "pT", "exp", "x2T", "score", "gexp", "combT")

            def pairs(g, qs, attention=False, prev=True):
                for q in qs:
                    silu(g, q)
                    if q >= HI_LAG:
                        high_part(g, q - HI_LAG)
                    elif prev:
                        high_part(g - 1, NQ - HI_LAG + q)
                    if attention and q == NQ - 1:
                        x_high(g + 1)
                    if q == LAG - 1 and prev:
                        y_copy(g - 1)
                    if q == RUN["keep"]:
                        keep(g)
                    if attention:
                        for name in NAMES:
                            if q == RUN[name]:
                                act_step(g + 1, name)

            for name in NAMES:
                act_step(0, name)
            x_high(0)
            pairs(0, range(HEAD), prev=False)
            with act.Fori(0, NG - 1) as g:
                pairs(g, range(HEAD, NQ), attention=True)
                pairs(g + 1, range(HEAD))
            pairs(NG - 1, range(HEAD, NQ))
            for q in range(NQ - HI_LAG, NQ):
                high_part(NG - 1, q)
            y_copy(NG - 1)

        @block.vector
        def _(dve):
            pre = [0]

            def setup(ins, wait=True):
                pre[0] += 1
                ins.then_inc(s_pre, 1)
                if wait:
                    dve.wait_ge(s_pre, pre[0])

            def vec(o):
                return steps[:, :, o - 64:o - 64 + C]

            dve.wait_ge(s_in, 48)
            setup(nc.vector.tensor_tensor(vec(O_V)[:, :, 1:C], x_sb[:, 1:, :], x_sb[:, 0:T, :], ALU.subtract), False)
            setup(nc.vector.tensor_tensor(vec(O_V)[:, :, 0], t_sb[:, 1:], t_sb[:, 0:T], ALU.subtract), False)
            setup(nc.vector.tensor_tensor(s1_sb[:, :, 1:C], x_sb[:, 0:T, :],
                                          x_sb[:, 0:1, :].to_broadcast([P, T, C - 1]), ALU.subtract), False)
            setup(nc.vector.tensor_scalar(s1_sb[:, :, 0], t_sb[:, 0:T], t_sb[:, 0:1], None, ALU.subtract), False)
            setup(nc.vector.memset(steps[:, :, O_ONE - 64], 1.0))
            setup(nc.vector.tensor_scalar(vec(O_VH), vec(O_V), 0.5, None, ALU.mult), False)
            setup(nc.vector.tensor_scalar(vec(O_VT), vec(O_V), 1.0 / 3.0, None, ALU.mult), False)
            setup(nc.vector.scalar_tensor_tensor(vec(O_E1), vec(O_V), 0.25, s1_sb[:], ALU.mult, ALU.add), False)
            setup(nc.vector.scalar_tensor_tensor(vec(O_D1), vec(O_V), 1.0 / 3.0, s1_sb[:], ALU.mult, ALU.add), False)
            setup(nc.vector.scalar_tensor_tensor(vec(O_C), vec(O_V), 0.5, s1_sb[:], ALU.mult, ALU.add))
            assert pre[0] == N_PRE
            for k in range(KT + 1):
                dve.wait_ge(s_rawhi, k + 1)
                n = P if k < KT else K5
                nc.vector.tensor_tensor(ws_lo[0:n, k, :], ws_raw[0:n, k % 2, :],
                                        ws_hi[0:n, k, :].bitcast(F32), ALU.subtract).then_inc(s_rawlo, 1)

            def outer(o, a, b, na):
                nb = b.shape[-1]
                return nc.vector.tensor_tensor(
                    o.rearrange("p (a b) -> p a b", a=na),
                    a.unsqueeze(2).to_broadcast([P, na, nb]),
                    b.unsqueeze(1).to_broadcast([P, na, nb]), ALU.mult)

            def factor(j, t):
                s = slot[:, j, :]
                dve.wait_ge(s_slot, t + 1)
                outer(small[:, 2, :], s[:, O_E1:O_E1 + C], s[:, O_VT:O_VT + C], C).then_inc(s_e, 1)
                dve.wait_ge(s_e, 3 * t + 1)
                dve.wait_ge(s_s2, t + 1)
                nc.vector.tensor_tensor(small[:, 3, :], s2r[:, j, :], small[:, 2, :], ALU.add).then_inc(s_e, 1)
                dve.wait_ge(s_e, 3 * t + 2)
                outer(e3[:], small[:, 3, :], s[:, O_VH:O_VH + C], C * C).then_inc(s_e, 1)
                dve.wait_ge(s_e, 3 * t + 3)
                dve.wait_ge(s_s3, t + 1)
                after(dve, s_ta, t)
                nc.vector.tensor_tensor(a_sb[:], s3r[:, j, :], e3[:], ALU.add).then_inc(s_a, 1)

            def low_parts(j, t):
                dve.wait_ge(s_athi, 2 * (t + 1))
                nc.vector.tensor_tensor(at_lo[:, j, 0:KT, :], ta_ps[:].rearrange("p (k b) -> p k b", k=KT),
                                        at_hi[:, j, 0:KT, :].bitcast(F32), ALU.subtract).then_inc(s_atlo, 1)
                nc.vector.tensor_tensor(at_lo[0:K5, j, KT, :], t5_ps[0:K5, 0:NB],
                                        at_hi[0:K5, j, KT, :].bitcast(F32), ALU.subtract).then_inc(s_atlo, 1)

            def tokens(i, j, t):
                after(dve, s_hst[j], 16 * i)
                for l in range(C):
                    if l % (C // HALVES) == 0:
                        dve.wait_ge(s_u, HALVES * t + l // (C // HALVES) + 1)
                    after(dve, s_acc, t * C + l)
                    prev = h_sb[:, (j - 1) % RING, :] if l == 0 else h_sb[:, j, :]
                    o = l % (C // HALVES) * D
                    nc.vector.scalar_tensor_tensor(
                        h_sb[:, j, :], u_ps[:, j, l // (C // HALVES), o:o + D],
                        slot[:, j, O_V + l:O_V + l + 1], prev, ALU.mult, ALU.add).then_inc(s_acc, 1)

            factor(0, 0)
            low_parts(0, 0)
            factor(1, 1)

            def body(i, j, t, last):
                if not last or j < RING - 1:
                    low_parts((j + 1) % RING, t + 1)
                if not last or j < RING - 2:
                    factor((j + 2) % RING, t + 2)
                tokens(i, j, t)

            for j in range(RING):
                body(0, j, j, False)
            with dve.Fori(0, T // RING - 2) as n:
                i = n + 1
                for j in range(RING):
                    body(i, j, i * RING + j, False)
            for j in range(RING):
                body(T // RING - 1, j, T - RING + j, True)

            dve.wait_ge(s_u, HALVES * T)
            dve.wait_ge(s_acc, C * T)
            dve.wait_ge(s_clo, CHUNKS)
            dve.wait_ge(s_s3, T + 1)
            for j in range(RING):
                dve.wait_ge(s_hst[j], 16 * (T // RING))
            nc.vector.memset(h_tok[:], 0.0)
            nc.vector.memset(att[:], 0.0)
            nc.vector.memset(yT[:], 0.0)
            nc.vector.memset(mhalf[:], -0.5).then_inc(s_yc, 1)
            nc.vector.memset(eps[:], EPS).then_inc(s_fin, 1)
            nc.vector.memset(spare[:], 0.0).then_inc(s_out, 1)
            nc.vector.memset(score[:], SENTINEL).then_inc(s_zero, 1)
            dve.wait_ge(s_zero, 1)

            def ts(o, i, a, b, op0, op1):
                return nc.vector.tensor_scalar(o, i, a, b, op0, op1)

            def norm_stats(g, src, first, base):
                for p in range(PT):
                    nc.vector.bn_stats(st[:, p, :], src[:, p, :]).then_inc(s_dv, 1)
                wait_apart(dve, s_dv, g * N_DV + base + PT, 0 if first else 1)
                for p in range(PT):
                    nc.vector.bn_aggr(mv[:, p, :], st[:, p, :]).then_inc(s_dv, 1)

            def normalise(g, src, norm):
                dve.wait_ge(s_rstd, g * 2 + norm + 1)
                for p in range(PT):
                    ts(xn[:, p, :], src[:, p, :], mv[:, p, 0:1], rstd[:, p:p + 1],
                       ALU.subtract, ALU.mult).then_inc(s_dv, 1)

            def dve_step(g, name):
                base = g * N_DV
                if name == "var1":
                    dve.wait_ge(s_load, g * 32 + 32)
                    norm_stats(g, h_tok, True, DV["var1"] - 8)
                if name == "xn1":
                    normalise(g, h_tok, 0)
                if name == "sub":
                    dve.wait_ge(s_pe, g * 8 + 4)
                    for b in range(2):
                        r = slice(b * TP, (b + 1) * TP)
                        sc = pb[r, :].rearrange("p (a q) -> p a q", a=PT)[:, :, b * TP:b * TP + T]
                        nc.vector.tensor_reduce(mx[r, :], sc, AX_X, ALU.max).then_inc(s_dv, 1)
                    for b in range(2):
                        r = slice(b * TP, (b + 1) * TP)
                        sc = pb[r, :].rearrange("p (a q) -> p a q", a=PT)[:, :, b * TP:b * TP + T]
                        dve.wait_ge(s_dv, base + DV["sub"] - 3 + b)
                        nc.vector.tensor_tensor(att[r, :, b * TP:b * TP + T], sc,
                                                mx[r, :].unsqueeze(2).to_broadcast([TP, PT, T]),
                                                ALU.subtract).then_inc(s_dv, 1)
                if name == "v":
                    dve.wait_ge(s_ac, g * 8 + AC["exp"])
                    for b in range(2):
                        r = slice(b * TP, (b + 1) * TP)
                        nc.vector.tensor_reduce(sm[r, :], att[r, :, b * TP:b * TP + T], AX_X,
                                                ALU.add).then_inc(s_dv, 1)
                    dve.wait_ge(s_dv, base + DV["v"] - 2)
                    nc.vector.reciprocal(rs[:], sm[:]).then_inc(s_dv, 1)
                    dve.wait_ge(s_dv, base + DV["v"] - 1)
                    dve.wait_ge(s_pe, g * 8 + 3)
                    nc.vector.tensor_tensor(v_sb[:], pa[:].rearrange("p (a o) -> p a o", a=PT),
                                            rs[:].unsqueeze(2).to_broadcast([P, PT, D]), ALU.mult).then_inc(s_dv, 1)
                if name == "h2":
                    dve.wait_ge(s_pe, g * 8 + 5)
                    after(dve, s_kept, g)
                    nc.vector.tensor_tensor(h2[:], pb[:].rearrange("p (a o) -> p a o", a=PT), h_tok[:],
                                            ALU.add).then_inc(s_dv, 1)
                if name == "var2":
                    dve.wait_ge(s_dv, base + DV["h2"])
                    norm_stats(g, h2, False, DV["var2"] - 8)
                if name == "xn2":
                    normalise(g, h2, 1)
                if name == "top":
                    wait_apart(dve, s_ac, g * 8 + AC["score"], 2)
                    for p in range(PT):
                        nc.vector.max(top[0:TT, p, :], score[0:TT, p, 0:NE]).then_inc(s_dv, 1)
                if name == "gsub":
                    dve.wait_ge(s_dv, base + DV["top"])
                    nc.vector.memset(top[0:TT, :, TOPK:8], SENTINEL).then_inc(s_dv, 1)
                    nc.vector.tensor_tensor(ex[0:TT], score[0:TT, :, 0:NE],
                                            top[0:TT, :, 0:1].to_broadcast([TT, PT, NE]),
                                            ALU.subtract).then_inc(s_dv, 1)
                if name == "taken":
                    wait_apart(dve, s_dv, base + DV["gsub"] - 1, 3)
                    for p in range(PT):
                        nc.vector.match_replace(taken[0:TT, p, :], top[0:TT, p, :], score[0:TT, p, :],
                                                -SENTINEL).then_inc(s_dv, 1)
                    dve.wait_ge(s_dv, base + DV["taken"] - 1)
                    nc.vector.tensor_tensor(mask[0:TT], taken[0:TT, :, 0:NE], score[0:TT, :, 0:NE],
                                            ALU.not_equal).then_inc(s_dv, 1)
                if name == "comb":
                    dve.wait_ge(s_dv, base + DV["taken"])
                    dve.wait_ge(s_ac, g * 8 + AC["gexp"])
                    k = DV["comb"]
                    nc.vector.tensor_tensor(mask[0:TT], mask[0:TT], ex[0:TT], ALU.mult).then_inc(s_dv, 1)
                    dve.wait_ge(s_dv, base + k - 3)
                    nc.vector.tensor_reduce(gsum[0:TT], mask[0:TT], AX_X, ALU.add).then_inc(s_dv, 1)
                    dve.wait_ge(s_dv, base + k - 2)
                    nc.vector.reciprocal(grs[0:TT], gsum[0:TT]).then_inc(s_dv, 1)
                    dve.wait_ge(s_dv, base + k - 1)
                    nc.vector.tensor_tensor(comb[0:TT], mask[0:TT], grs[0:TT].unsqueeze(2).to_broadcast([TT, PT, NE]),
                                            ALU.mult).then_inc(s_dv, 1)

            NAMES = ("var1", "xn1", "sub", "v", "h2", "var2", "xn2", "top", "gsub", "taken", "comb")

            def x_low(g):
                dve.wait_ge(s_xhi, g + 1)
                nc.vector.tensor_tensor(x_lo[:], x2n[:], x_hi[:].bitcast(F32), ALU.subtract).then_inc(s_xlo, 1)

            def hidden(g, q):
                n = g * NQ + q
                dve.wait_ge(s_x3, n + 1)
                if q < 2:
                    dve.wait_ge(s_silu, n + 1)
                    factor = sig[:, q % 2, :]
                else:
                    dve.wait_ge(s_sc, g * (NQ - 2) + q - 1)
                    factor = scaled[:, q % 2, :]
                after(dve, s_lo, last_use(HID_SLOT, g, q))
                nc.vector.tensor_tensor(hid[:, HID_SLOT[q], :], x3_ps[:, X3_SLOT[q], 0:GT], factor,
                                        ALU.mult).then_inc(s_h, 1)

            def low_part(g, q):
                dve.wait_ge(s_hi, g * NQ + q + 1)
                k = HID_SLOT[q]
                nc.vector.tensor_tensor(hid_lo[:, k, :], hid[:, k, :], hid_hi[:, k, :].bitcast(F32),
                                        ALU.subtract).then_inc(s_lo, 1)

            def finish(g):
                dve.wait_ge(s_yt, g + 1)
                dve.wait_ge(s_kept, g + 1)
                dve.wait_ge(s_out, g * 32 + 1)
                nc.vector.tensor_tensor(y_sb[:], pa[:].rearrange("p (a o) -> p a o", a=PT), h2_kept[:],
                                        ALU.add).then_inc(s_fin, 1)

            def pairs(g, qs, attention=False, prev=True):
                for q in qs:
                    hidden(g, q)
                    if attention:
                        for name in NAMES:
                            if q == RUN[name]:
                                dve_step(g + 1, name)
                    if q >= LO_LAG:
                        low_part(g, q - LO_LAG)
                    elif prev:
                        low_part(g - 1, NQ - LO_LAG + q)
                    if attention and q == NQ - 2:
                        x_low(g + 1)
                    if q == HEAD - 1 and prev:
                        finish(g - 1)

            for name in NAMES:
                dve_step(0, name)
            x_low(0)
            pairs(0, range(HEAD), prev=False)
            with dve.Fori(0, NG - 1) as g:
                pairs(g, range(HEAD, NQ), attention=True)
                pairs(g + 1, range(HEAD))
            pairs(NG - 1, range(HEAD, NQ))
            for q in range(NQ - LO_LAG, NQ):
                low_part(NG - 1, q)
            finish(NG - 1)

        @block.tensor
        def _(pe):
            def three(o, lhs_hi, lhs_lo, rhs_hi, rhs_lo, first=True, last=True):
                nc.tensor.matmul(o, lhs_hi, rhs_hi, start=first, stop=False)
                nc.tensor.matmul(o, lhs_lo, rhs_hi, start=False, stop=False)
                return nc.tensor.matmul(o, lhs_hi, rhs_lo, start=False, stop=last)

            def transposes(j, t):
                pe.wait_ge(s_a, t + 1)
                pe.wait_ge(s_b, t + 1)
                after(pe, s_atlo, 2 * t)
                for k in range(KT):
                    nc.tensor.transpose(ta_ps[:, k * P:(k + 1) * P], a_sb[:, k * P:(k + 1) * P], ident[:])
                nc.tensor.transpose(t5_ps[0:K5, 0:NB], slot[:, j, 0:K5], ident[:]).then_inc(s_ta, 1)

            def project(j, t, first=False):
                pe.wait_ge(s_atlo, 2 * (t + 1))
                if not isinstance(t, int) or t >= RING:
                    pe.wait_ge(s_acc, (t - RING + 1) * C)
                for h in range(HALVES):
                    cols = slice(h * (NU // HALVES), (h + 1) * (NU // HALVES))
                    for k in range(KT + 1):
                        if first and h == 0:
                            pe.wait_ge(s_rawlo, k + 1)
                        n = P if k < KT else K5
                        mm = three(u_ps[:, j, h, :], at_hi[0:n, j, k, :], at_lo[0:n, j, k, :],
                                   ws_hi[0:n, k, cols], ws_lo[0:n, k, cols], k == 0, k == KT)
                    mm.then_inc(s_u, 1)

            pe.wait_ge(s_id, 2)
            transposes(0, 0)
            for t in range(RING):
                transposes((t + 1) % RING, t + 1)
                project(t, t, t == 0)
            with pe.Fori(0, T // RING - 2) as n:
                i = n + 1
                for j in range(RING):
                    transposes((j + 1) % RING, i * RING + j + 1)
                    project(j, i * RING + j)
            for t in range(T - RING, T):
                if t + 1 < T:
                    transposes((t + 1) % RING, t + 1)
                project(t % RING, t)

            pe.wait_ge(s_wqk, 64)
            pe.wait_ge(s_acc, C * T)
            nc.tensor.matmul(pa[:, 0:D], wq_sb[:], wk_sb[:], start=True, stop=True).then_inc(s_qk, 1)
            pe.wait_ge(s_qk, 2)

            def group(g, o, pairs):
                for p in range(PT):
                    lhs, rhs = pairs(p)
                    mm = nc.tensor.matmul(o[:, p, :], lhs, rhs, start=True, stop=True)
                return mm.then_inc(s_pe, 1)

            def transpose_group(src, bank):
                for p in range(PT):
                    mm = nc.tensor.transpose(bank[:, p * P:(p + 1) * P], src[:, p, :], ident[:])
                return mm

            pa3 = pa[:].rearrange("p (a q) -> p a q", a=PT)
            pb3 = pb[:].rearrange("p (a q) -> p a q", a=PT)

            def pe_step(g, name):
                base = g * N_DV
                if name == "pe_xnT":
                    pe.wait_ge(s_dv, base + DV["xn1"])
                    after(pe, s_fin, g)
                    transpose_group(xn, pa).then_inc(s_pe, 1)
                if name == "pe_pT":
                    pe.wait_ge(s_ac, g * 8 + AC["xnT"])
                    after(pe, s_ac, g * 8)
                    nc.tensor.matmul(pb[:], qk_sb[:], xnT[:].rearrange("p a b -> p (a b)"), start=True,
                                     stop=True).then_inc(s_pe, 1)
                    group(g, pa3, lambda p: (xnT[:, p, :], wv_sb[:]))
                if name == "pe_score":
                    pe.wait_ge(s_ac, g * 8 + AC["pT"])
                    group(g, pb3, lambda p: (xnT[:, p, :], pT[:, p, :]))
                if name == "pe_out":
                    pe.wait_ge(s_dv, base + DV["v"])
                    group(g, pb3, lambda p: (att[:, p, :], v_sb[:, p, :]))
                if name == "pe_x2T":
                    pe.wait_ge(s_dv, base + DV["xn2"])
                    transpose_group(xn, pa).then_inc(s_pe, 1)
                if name == "pe_gate":
                    pe.wait_ge(s_ac, g * 8 + AC["x2T"])
                    for p in range(PT):
                        mm = nc.tensor.matmul(pa[0:TT, p * NE:(p + 1) * NE], x2n[:, p * TT:(p + 1) * TT],
                                              wg_sb[:], start=True, stop=True)
                    mm.then_inc(s_pe, 1)
                if name == "pe_combT":
                    pe.wait_ge(s_dv, base + DV["comb"])
                    for a in range(PT // 2):
                        mm = nc.tensor.transpose(pb[:, a * TT:(a + 1) * TT],
                                                 comb[0:TT, 2 * a:2 * a + 2].rearrange("p a e -> p (a e)"),
                                                 ident[0:TT, 0:TT])
                    mm.then_inc(s_pe, 1)

            NAMES = ("pe_xnT", "pe_pT", "pe_score", "pe_out", "pe_x2T", "pe_gate", "pe_combT")

            def w(kind, q, part):
                c = (kind * NQ + q) * P
                return part[:, c:c + P]

            def x1_hi(g, q):
                after(pe, s_silu, g * NQ + q - 1)
                o = x1_ps[:, q % 2, 0:GT]
                nc.tensor.matmul(o, w(0, q, w_hi), x_hi[:], start=True, stop=False)
                nc.tensor.matmul(o, w(0, q, w_lo), x_hi[:], start=False, stop=False)

            def x3_hi(g, q):
                after(pe, s_h, last_use(X3_SLOT, g, q))
                o = x3_ps[:, X3_SLOT[q], 0:GT]
                nc.tensor.matmul(o, w(1, q, w_hi), x_hi[:], start=True, stop=False)
                nc.tensor.matmul(o, w(1, q, w_lo), x_hi[:], start=False, stop=False)

            def x1_lo(g, q):
                nc.tensor.matmul(x1_ps[:, q % 2, 0:GT], w(0, q, w_hi), x_lo[:], start=False,
                                 stop=True).then_inc(s_x1, 1)

            def x3_lo(g, q):
                nc.tensor.matmul(x3_ps[:, X3_SLOT[q], 0:GT], w(1, q, w_hi), x_lo[:], start=False,
                                 stop=True).then_inc(s_x3, 1)

            def up(g, q):
                if q == 0:
                    pe.wait_ge(s_xhi, g + 1)
                    x1_hi(g, q)
                    x3_hi(g, q)
                    pe.wait_ge(s_xlo, g + 1)
                    x1_lo(g, q)
                    x3_lo(g, q)
                else:
                    x1_hi(g, q)
                    x1_lo(g, q)
                    x3_hi(g, q)
                    x3_lo(g, q)

            def down(g, q):
                n = g * NQ + q
                k = HID_SLOT[q]
                o = y_ps[:, 0:GT]
                pe.wait_ge(s_hi, n + 1)
                if q == 0:
                    pe.wait_ge(s_yc, g + 1)
                nc.tensor.matmul(o, w(2, q, w_hi), hid_hi[:, k, :], start=q == 0, stop=False)
                nc.tensor.matmul(o, w(2, q, w_lo), hid_hi[:, k, :], start=False, stop=False)
                pe.wait_ge(s_lo, n + 1)
                nc.tensor.matmul(o, w(2, q, w_hi), hid_lo[:, k, :], start=False, stop=q == NQ - 1).then_inc(s_y, 1)

            def y_transpose(g):
                pe.wait_ge(s_yc, g + 2)
                for p in range(PT):
                    mm = nc.tensor.transpose(pa[:, p * D:(p + 1) * D], yT[:, p].rearrange("p b t -> p (b t)"),
                                             ident[:])
                mm.then_inc(s_yt, 1)

            def pairs(g, qs, attention=False, prev=True):
                for q in qs:
                    if q == 0 and prev:
                        down(g - 1, NQ - LAG)
                    up(g, q)
                    if q >= LAG:
                        down(g, q - LAG)
                    elif q > 0 and prev:
                        down(g - 1, NQ - LAG + q)
                    if q == HEAD - 2 and prev:
                        pe.wait_ge(s_ac, g * 8 + AC["score"])
                        y_transpose(g - 1)
                    if attention:
                        for name in NAMES:
                            if q == RUN[name]:
                                pe_step(g + 1, name)

            for name in NAMES:
                pe_step(0, name)
            pe.wait_ge(s_clo, CHUNKS)
            pairs(0, range(HEAD), prev=False)
            with pe.Fori(0, NG - 1) as g:
                pairs(g, range(HEAD, NQ), attention=True)
                pairs(g + 1, range(HEAD))
            pairs(NG - 1, range(HEAD, NQ))
            for q in range(NQ - LAG, NQ):
                down(NG - 1, q)
            y_transpose(NG - 1)


HID_SLOTS = 5
HID_SLOT = [q % HID_SLOTS for q in range(NQ)]
X3_SLOT = [q % 3 for q in range(NQ - 1)] + [1]
HI_LAG, LO_LAG = 2, 1
N_PRE = 10
DV = {}
_n = 0
for _name, _ops in (("var1", 8), ("xn1", 4), ("sub", 4), ("v", 4), ("h2", 1), ("var2", 8), ("xn2", 4),
                    ("top", 4), ("gsub", 2), ("taken", 5), ("comb", 4)):
    _n += _ops
    DV[_name] = _n
N_DV = _n
AC = {"xnT": 1, "pT": 2, "exp": 4, "x2T": 5, "score": 6, "gexp": 7, "combT": 8}
RUN = {"keep": 7, "var1": 7, "rstd1": 8, "xn1": 8, "pe_xnT": 10, "xnT": 10, "pe_pT": 11, "pT": 11,
       "pe_score": 12, "sub": 12, "exp": 14, "v": 14, "pe_out": 16, "h2": 16, "var2": 17, "rstd2": 18,
       "xn2": 18, "pe_x2T": 20, "x2T": 20, "pe_gate": 21, "score": 21, "top": 22, "gsub": 23, "taken": 24,
       "gexp": 25, "comb": 26, "pe_combT": 28, "combT": 28}


def kernel(x, L0_tok_W, L0_tok_b, L0_attn_Wq, L0_attn_Wk, L0_attn_Wv, L0_ffn_w_gate, L0_ffn_w1, L0_ffn_w2,
           L0_ffn_w3, L0_ffn_w_sg, L0_ffn_w_su, L0_ffn_w_sd):
    import numpy as np
    import concourse.bacc as bacc
    from concourse.bass_utils import run_bass_kernel_spmd

    ffw = np.concatenate([
        np.transpose(L0_ffn_w_sg), np.transpose(L0_ffn_w1, (2, 0, 1)).reshape(D, -1),
        np.transpose(L0_ffn_w_su), np.transpose(L0_ffn_w3, (2, 0, 1)).reshape(D, -1),
        np.transpose(np.concatenate([np.transpose(L0_ffn_w_sd), np.asarray(L0_ffn_w2).reshape(-1, D)])
                     .reshape(NQ, P, D), (1, 0, 2)).reshape(P, -1)], axis=1)
    arrays = {
        "x": np.asarray(x).reshape(NB, -1),
        "tgrid": np.linspace(0.0, 1.0, T + 1, dtype=np.float32).reshape(1, -1),
        "wt": np.transpose(L0_tok_W), "bias": np.asarray(L0_tok_b).reshape(1, -1),
        "wq": L0_attn_Wq, "wk": L0_attn_Wk, "wvt": np.transpose(L0_attn_Wv),
        "wgt": np.transpose(L0_ffn_w_gate), "ffw": ffw}
    arrays = {k: np.ascontiguousarray(a) for k, a in arrays.items()}
    nc = bacc.Bacc("TRN2", target_bir_lowering=False, num_devices=1)
    args = [nc.dram_tensor(k, a.shape, mybir.dt.from_np(a.dtype), kind="ExternalInput").ap()
            for k, a in arrays.items()]
    out = nc.dram_tensor("out", (NB * T, D), F32, kind="ExternalOutput").ap()
    audio_tower(nc, *args, out)
    r = run_bass_kernel_spmd(nc, [arrays], core_ids=[0])
    return r.results[0]["out"].reshape(NB, T, D)
```

```python
from contextlib import ExitStack

import concourse.bass as bass
from concourse import mybir

F32 = mybir.dt.float32
F32R = mybir.dt.float32r
ALU = mybir.AluOpType
ACT = mybir.ActivationFunctionType
AX_X = mybir.AxisListType.X

P = 128
NB = 128
T = 63
C = 8
D = 128
NE = 64
TOPK = 6
KT = C ** 3 // P
BC = C * C
C1 = C + 1
NU = C * D
RING = 3
HALVES = 2
GB = 8
NG = NB // GB
PT = GB // 2
TP = 64
GT = GB * T
TT = 2 * T
NQ = 2 + NE // 2
LAG = 4
BATCH = 4
NBATCH = (NQ - 2) // BATCH
HEAD = 7
WCOLS = 3 * NQ * P
CHUNKS = 16
CH = WCOLS // CHUNKS
EPS = 1e-5
SENTINEL = 3.0e38
C1_STEP = 16
O_C1 = 2 * BC
O_C = O_C1 + 1
O_V = 3 * BC
O_VH, O_VT, O_E1, O_D1 = (O_V + k * C for k in range(1, 5))
SLOT = O_V + 5 * C
K_ONE, K_C = 0, 1
K_V, K_VH, K_VT, K_E1, K_D1 = (C1 + k * C for k in range(5))
PK = C1 + 5 * C
RAW = 3
X, Y = KT, KT + 1
ORDER = (0, 1, Y, 2, 3, X)
N_LO = {0: 1, 1: 2, Y: 4, 2: 5, 3: 6}
N_DV = 47


def audio_tower(nc, x, tgrid, wt, bias, wq, wk, wvt, wgt, ffw, out):
    h_dram = nc.dram_tensor("h_tokens", (NB, T, D), F32).ap()
    comb_dram = nc.dram_tensor("routing_weights", (NG, NE, GT), F32).ap()
    comb_store = comb_dram.rearrange("g e (a h t) -> g h e a t", h=2, t=TT)
    h_load = h_dram.rearrange("(g p b) t o -> g b t p o", p=PT, b=2)
    out_rows = out.rearrange("(g p b t) o -> g b t p o", p=PT, b=2, t=T)

    with ExitStack() as ctx:
        def sem(name):
            return ctx.enter_context(nc.semaphore(name))

        def sb(name, shape, dt=F32, scope=ctx):
            return scope.enter_context(nc.sbuf_tensor(name, shape, dt))

        ident = sb("ident", [P, P])
        w_hi = sb("w_hi", [P, WCOLS], F32R)
        w_lo = sb("w_lo", [P, WCOLS], F32R)
        wq_sb = sb("wq_sb", [P, D])
        wk_sb = sb("wk_sb", [P, D])
        wv_sb = sb("wv_sb", [P, D])
        wg_sb = sb("wg_sb", [P, NE])
        qk_sb = sb("qk_sb", [P, D])
        s1 = ExitStack()
        p1 = ExitStack()
        ws_hi = sb("ws_hi", [P, KT, NU], F32R, s1)
        ws_lo = sb("ws_lo", [P, KT, NU], F32R, s1)
        ws_xy = sb("ws_xy", [P, 2, NU], F32R, s1)
        ws_raw = sb("ws_raw", [P, RAW, NU], F32, s1)
        s1_sb = sb("s1_sb", [P, T, C], F32, s1)
        steps = sb("steps", [P, T, PK], F32, s1)
        slot = sb("slot", [P, RING, SLOT], F32, s1)
        s2r = sb("s2r", [P, RING, C * C], F32, s1)
        s3r = sb("s3r", [P, RING, C ** 3], F32, s1)
        small = sb("small", [P, 4, C * C], F32, s1)
        b3 = sb("b3", [P, C ** 3], F32, s1)
        e3 = sb("e3", [P, C ** 3], F32, s1)
        a_sb = sb("a_sb", [P, C ** 3], F32, s1)
        at_hi = sb("at_hi", [P, RING, KT, NB], F32R, s1)
        at_lo = sb("at_lo", [P, RING, KT, NB], F32R, s1)
        at_xy = sb("at_xy", [P, RING, 2, NB], F32R, s1)
        h_sb = sb("h_sb", [P, RING, D], F32, s1)
        chunk = sb("chunk", [P, CH], F32, s1)
        x_sb = chunk[:, 0:(T + 1) * (C - 1)].rearrange("p (t c) -> p t c", t=T + 1)
        t_sb = chunk[:, (T + 1) * (C - 1):(T + 1) * C]
        u_ps = p1.enter_context(nc.psum_tensor("u_ps", [P, RING, HALVES, NU // HALVES], F32))
        ta_ps = p1.enter_context(nc.psum_tensor("ta_ps", [P, C ** 3], F32))
        t5_ps = p1.enter_context(nc.psum_tensor("t5_ps", [P, 512], F32))
        s1.close()
        p1.close()
        h_tok = sb("h_tok", [P, PT, D])
        st = sb("st", [P, PT, 6])
        mv = sb("mv", [P, PT, 2])
        vare = sb("vare", [P, PT])
        rstd = sb("rstd", [P, PT])
        mhalf = sb("mhalf", [P, PT])
        eps = sb("eps", [P, PT])
        xn = sb("xn", [P, PT, D])
        xnT = sb("xnT", [P, PT, P])
        pT = sb("pT", [P, PT, P])
        att = sb("att", [P, PT, P])
        mx = sb("mx", [P, PT])
        sm = sb("sm", [P, PT])
        rs = sb("rs", [P, PT])
        v_sb = sb("v_sb", [P, PT, D])
        h2 = sb("h2", [P, PT, D])
        x2n = sb("x2n", [P, GT])
        h2_kept = sb("h2_kept", [P, PT, D])
        combT = sb("combT", [P, PT // 2, TT])
        score = sb("score", [P, PT, NE + 2])
        taken = sb("taken", [P, PT, NE + 2])
        top = sb("top", [P, PT, 8])
        ex = sb("ex", [P, PT, NE])
        mask = sb("mask", [P, PT, NE])
        spare = sb("spare", [P, 4])
        gsum = sb("gsum", [P, PT])
        grs = sb("grs", [P, PT])
        comb = sb("comb", [P, PT, NE])
        x_hi = sb("x_hi", [P, GT], F32R)
        x_lo = sb("x_lo", [P, GT], F32R)
        cbb = sb("cbb", [P, 2, BATCH, GT])
        sig = sb("sig", [P, 2, GT])
        scaled = sb("scaled", [P, 2, GT])
        hid = sb("hid", [P, HID_SLOTS, GT])
        hid_hi = sb("hid_hi", [P, HID_SLOTS, GT], F32R)
        hid_lo = sb("hid_lo", [P, HID_SLOTS, GT], F32R)
        yT = sb("yT", [P, PT, 2, TP])
        y_sb = sb("y_sb", [P, PT, D])
        x1_ps = ctx.enter_context(nc.psum_tensor("x1_ps", [P, 2, 512], F32))
        x3_ps = ctx.enter_context(nc.psum_tensor("x3_ps", [P, 3, 512], F32))
        y_ps = ctx.enter_context(nc.psum_tensor("y_ps", [P, 512], F32))
        pa = ctx.enter_context(nc.psum_tensor("pa", [P, 512], F32))
        pb = ctx.enter_context(nc.psum_tensor("pb", [P, 512], F32))

        s_in = sem("s_in")
        s_wqk = sem("s_wqk")
        s_raw = [sem(f"s_raw{k}") for k in range(RAW)]
        s_clear = sem("s_clear")
        s_move = sem("s_move")
        s_rawhi = sem("s_rawhi")
        s_rawlo = sem("s_rawlo")
        s_chunk = sem("s_chunk")
        s_chi = sem("s_chi")
        s_clo = sem("s_clo")
        s_id = sem("s_id")
        s_pre = sem("s_pre")
        s_slot = sem("s_slot")
        s_pool = sem("s_pool")
        s_b = sem("s_b")
        s_s2 = sem("s_s2")
        s_s3 = sem("s_s3")
        s_e = sem("s_e")
        s_a = sem("s_a")
        s_ta = sem("s_ta")
        s_athi = sem("s_athi")
        s_atlo = sem("s_atlo")
        s_u = sem("s_u")
        s_acc = sem("s_acc")
        s_hst = [sem(f"s_hst{j}") for j in range(RING)]
        s_load = sem("s_load")
        s_dv = sem("s_dv")
        s_rstd = sem("s_rstd")
        s_veps = sem("s_veps")
        s_pe = sem("s_pe")
        s_ac = sem("s_ac")
        s_zero = sem("s_zero")
        s_qk = sem("s_qk")
        s_xhi = sem("s_xhi")
        s_xlo = sem("s_xlo")
        s_comb = sem("s_comb")
        s_cbb = [sem("s_cbb0"), sem("s_cbb1")]
        s_x1 = sem("s_x1")
        s_x3 = sem("s_x3")
        s_y = sem("s_y")
        s_silu = sem("s_silu")
        s_sc = sem("s_sc")
        s_h = sem("s_h")
        s_hi = sem("s_hi")
        s_lo = sem("s_lo")
        s_yc = sem("s_yc")
        s_yt = sem("s_yt")
        s_fin = sem("s_fin")
        s_kept = sem("s_kept")
        s_out = sem("s_out")

        def after(eng, s, value):
            if not isinstance(value, int) or value > 0:
                eng.wait_ge(s, value)

        def last_use(slots, g, q):
            d = 1
            while slots[(q - d) % NQ] != slots[q]:
                d += 1
            return g * NQ + q - d + 1

        def wait_apart(eng, s, value, place):
            eng.wait_ge(s, value)
            nc.vector.memset(spare[:, place:place + 1], 0.0)

        block = ctx.enter_context(nc.Block())

        @block.sync
        def _(sp):
            sp.dma_start(x_sb, x.rearrange("p (t c) -> p t c", t=T + 1)).then_inc(s_in, 16)
            sp.dma_start(t_sb, tgrid.to_broadcast([P, T + 1])).then_inc(s_in, 16)
            sp.dma_start(h_sb[:, RING - 1, :], bias.to_broadcast([P, D])).then_inc(s_in, 16)
            w4 = wt[C + C * C + C ** 3:, :].rearrange("(k p l) o -> k p (l o)", k=KT, l=C)
            rows_b = wt[C + BC:C + BC + C * BC, :].rearrange("(p l) o -> p (l o)", l=C)
            rows_c1 = wt[0:C + BC, :].rearrange("(p l) o -> p (l o)", l=C)

            def load_tile(k):
                raw, landed = ws_raw[:, ORDER.index(k) % RAW, :], s_raw[ORDER.index(k) % RAW]
                if k < KT:
                    sp.dma_start(raw, w4[k]).then_inc(landed, 16)
                if k == X:
                    for b in range(2):
                        sp.dma_start(raw[b * BC:(b + 1) * BC], rows_b).then_inc(landed, 16)
                if k == Y:
                    sp.wait_ge(s_clear, 1)
                    sp.dma_start(raw[0:BC], rows_b).then_inc(landed, 16)
                    for r in range(BC, BC + 3 * C1_STEP, C1_STEP):
                        sp.dma_start(raw[r:r + C1], rows_c1).then_inc(landed, 16)

            load_tile(0)
            load_tile(1)
            load_tile(Y)
            sp.wait_ge(s_rawlo, N_LO[0])
            load_tile(2)
            sp.wait_ge(s_rawlo, N_LO[1])
            load_tile(3)
            sp.wait_ge(s_rawlo, N_LO[Y])
            y_raw = ws_raw[:, ORDER.index(Y) % RAW, :]
            sp.dma_start(ws_xy[BC + C1_STEP:BC + C1_STEP + C1, 1, :].bitcast(F32),
                         y_raw[BC:BC + C1]).then_inc(s_move, 16)
            sp.wait_ge(s_move, 16)
            load_tile(X)
            sp.dma_start(wq_sb[:], wq).then_inc(s_wqk, 16)
            sp.dma_start(wk_sb[:], wk).then_inc(s_wqk, 16)
            sp.dma_start(wv_sb[:], wvt).then_inc(s_wqk, 16)
            sp.dma_start(wg_sb[:], wgt).then_inc(s_wqk, 16)

            sp.wait_ge(s_pre, N_PRE)

            def load_chunk(i):
                after(sp, s_clo, i)
                sp.dma_start(chunk[:], ffw[:, bass.ds(i * CH, CH)]).then_inc(s_chunk, 16)

            def store_h(i, j, t, last):
                sp.wait_ge(s_acc, (t + 1) * C)
                sp.dma_start(h_dram[:, t, :], h_sb[:, j, :]).then_inc(s_hst[j], 16)

            load_chunk(0)
            with sp.Fori(0, CHUNKS - 1) as i:
                for j in range(RING):
                    store_h(i, j, i * RING + j, False)
                load_chunk(i + 1)
            with sp.Fori(0, T // RING - CHUNKS + 1) as n:
                i = n + CHUNKS - 1
                for j in range(RING):
                    store_h(i, j, i * RING + j, False)

            def load_group(g):
                for b in range(2):
                    sp.dma_start(h_tok[b * TP:b * TP + T, :, :], h_load[g, b]).then_inc(s_load, 16)

            def store_group(g):
                sp.wait_ge(s_fin, g + 2)
                for b in range(2):
                    sp.dma_start(out_rows[g, b], y_sb[b * TP:b * TP + T, :, :]).then_inc(s_out, 16)

            for j in range(RING):
                sp.wait_ge(s_hst[j], 16 * (T // RING))
            sp.wait_ge(s_zero, 1)
            load_group(0)
            sp.wait_ge(s_dv, DV["h2"])
            load_group(1)

            def store_comb(g):
                sp.wait_ge(s_ac, g * 8 + AC["combT"])
                for h in range(2):
                    sp.dma_start(comb_store[g, h], combT[h * NE:(h + 1) * NE, :, :]).then_inc(s_comb, 16)

            def load_batch(g, k, wait=True):
                if k == 0:
                    sp.wait_ge(s_comb, (g + 1) * 32)
                if wait:
                    sp.wait_ge(s_sc, g * (NQ - 2) + (k - 1) * BATCH)
                e = 2 * BATCH * k
                for b in range(2):
                    rows = comb_dram[g, e + b:e + 2 * BATCH:2, :]
                    sp.dma_start(cbb[b * NE:(b + 1) * NE, k % 2, :, :],
                                 rows.unsqueeze(0).to_broadcast([NE, BATCH, GT])).then_inc(s_cbb[k % 2], 16)

            def first_batches(g, wait):
                store_comb(g)
                load_batch(g, 0, wait)
                load_batch(g, 1, wait)
                load_batch(g, 2)

            first_batches(0, False)
            with sp.Fori(0, NG - 2) as g:
                for k in range(3, NBATCH):
                    load_batch(g, k)
                    if k == 5:
                        sp.wait_ge(s_dv, (g + 1) * N_DV + DV["h2"])
                        load_group(g + 2)
                first_batches(g + 1, True)
                store_group(g)
            for g in range(NG - 2, NG):
                for k in range(3, NBATCH):
                    load_batch(g, k)
                if g + 1 < NG:
                    first_batches(g + 1, True)
                store_group(g)
            sp.wait_ge(s_out, 32 * NG + 1)

        @block.gpsimd
        def _(pool):
            nc.gpsimd.memset(ident[:], 0.0).then_inc(s_id, 1)
            pool.wait_ge(s_id, 1)
            nc.gpsimd.affine_select(out=ident[:], in_=ident[:], compare_op=ALU.not_equal, fill=1.0, base=0,
                                    pattern=[[-1, P]], channel_multiplier=1).then_inc(s_id, 1)
            nc.gpsimd.memset(s2r[:, 0, :], 0.0).then_inc(s_s2, 1)
            nc.gpsimd.memset(s3r[:, 0, :], 0.0).then_inc(s_s3, 1)
            pool.wait_ge(s_pre, N_PRE)
            pool.wait_ge(s_clear, 2)

            def outer(o, a, b, na):
                nb = b.shape[-1]
                return nc.gpsimd.tensor_tensor(
                    o.rearrange("p (a b) -> p a b", a=na),
                    a.unsqueeze(2).to_broadcast([P, na, nb]),
                    b.unsqueeze(1).to_broadcast([P, na, nb]), ALU.mult)

            def state(i, j, t, last):
                nx = (j + 1) % RING
                s = slot[:, j, :]
                after(pool, s_acc, (t - RING + 1) * C if not isinstance(t, int) or t >= RING else 0)
                nc.gpsimd.tensor_copy(s[:, O_V:SLOT], steps[:, t, K_V:PK]).then_inc(s_slot, 1)
                nc.gpsimd.tensor_copy(
                    s[:, O_C1:O_C1 + 3 * C1_STEP].rearrange("p (r c) -> p r c", c=C1_STEP)[:, :, 0:C1],
                    steps[:, t, 0:C1].unsqueeze(1).to_broadcast([P, 3, C1])).then_inc(s_slot, 1)
                pool.wait_ge(s_slot, 2 * t + 2)
                outer(small[:, 0, :], s[:, O_D1:O_D1 + C], s[:, O_VH:O_VH + C], C).then_inc(s_pool, 1)
                outer(small[:, 1, :], s[:, O_C:O_C + C], s[:, O_V:O_V + C], C).then_inc(s_pool, 1)
                pool.wait_ge(s_pool, 3 * t + 1)
                pool.wait_ge(s_s2, t + 1)
                nc.gpsimd.tensor_tensor(s[:, 0:2 * BC].rearrange("p (r c) -> p r c", r=2),
                                        s2r[:, j, :].unsqueeze(1).to_broadcast([P, 2, BC]),
                                        small[:, 0, :].unsqueeze(1).to_broadcast([P, 2, BC]),
                                        ALU.add).then_inc(s_b, 1)
                pool.wait_ge(s_pool, 3 * t + 2)
                pool.wait_ge(s_a, t - 1) if not isinstance(t, int) or t > 1 else None
                nc.gpsimd.tensor_tensor(s2r[:, nx, :], s2r[:, j, :], small[:, 1, :], ALU.add).then_inc(s_s2, 1)
                pool.wait_ge(s_b, t + 1)
                outer(b3[:], s[:, 0:BC], s[:, O_V:O_V + C], C * C).then_inc(s_pool, 1)
                pool.wait_ge(s_pool, 3 * t + 3)
                pool.wait_ge(s_s3, t + 1)
                nc.gpsimd.tensor_tensor(s3r[:, nx, :], s3r[:, j, :], b3[:], ALU.add).then_inc(s_s3, 1)

            def split_chunk(i):
                pool.wait_ge(s_chi, i + 1)
                nc.gpsimd.tensor_tensor(w_lo[:, bass.ds(i * CH, CH)], chunk[:],
                                        w_hi[:, bass.ds(i * CH, CH)].bitcast(F32), ALU.subtract).then_inc(s_clo, 1)

            for t in range(2):
                state(0, t, t, False)
            state(0, 2, 2, False)
            split_chunk(0)
            with pool.Fori(0, CHUNKS - 1) as n:
                i = n + 1
                for j in range(RING):
                    state(i, j, i * RING + j, False)
                split_chunk(i)
            with pool.Fori(0, T // RING - CHUNKS) as n:
                i = n + CHUNKS
                for j in range(RING):
                    state(i, j, i * RING + j, False)

            pool.wait_ge(s_zero, 1)

            def inverse_std(g, norm):
                pool.wait_ge(s_dv, g * N_DV + DV["var1" if norm == 0 else "var2"])
                nc.gpsimd.tensor_tensor(vare[:], mv[:, :, 1], eps[:], ALU.add).then_inc(s_veps, 1)
                pool.wait_ge(s_veps, g * 2 + norm + 1)
                nc.gpsimd.tensor_tensor(rstd[:], vare[:], mhalf[:], ALU.pow).then_inc(s_rstd, 1)

            def scale(g, q):
                n = g * NQ + q
                k = (q - 2) // BATCH
                pool.wait_ge(s_silu, n + 1)
                pool.wait_ge(s_cbb[k % 2], 32 * (g * (NBATCH // 2) + k // 2 + 1))
                after(pool, s_h, n - 1)
                nc.gpsimd.tensor_tensor(scaled[:, q % 2, :], sig[:, q % 2, :], cbb[:, k % 2, (q - 2) % BATCH, :],
                                        ALU.mult).then_inc(s_sc, 1)

            def pairs(g, qs, attention=False, prev=True):
                for q in qs:
                    if q >= 2:
                        scale(g, q)
                    if attention and q == RUN["rstd1"]:
                        inverse_std(g + 1, 0)
                    if attention and q == RUN["rstd2"]:
                        inverse_std(g + 1, 1)

            inverse_std(0, 0)
            inverse_std(0, 1)
            pairs(0, range(HEAD), prev=False)
            with pool.Fori(0, NG - 1) as g:
                pairs(g, range(HEAD, NQ), attention=True)
                pairs(g + 1, range(HEAD))
            pairs(NG - 1, range(HEAD, NQ))

        @block.scalar
        def _(act):
            def split_tile(k):
                n = ORDER.index(k)
                act.wait_ge(s_raw[n % RAW], {0: 16, 1: 16, Y: 64, 2: 32, 3: 32, X: 96}[k])
                o = ws_hi[:, k, :] if k < KT else ws_xy[:, k - KT, :]
                nc.scalar.activation(o, ws_raw[:, n % RAW, :], ACT.Copy).then_inc(s_rawhi, 1)

            def high_parts(j, t):
                act.wait_ge(s_ta, t + 1)
                if not isinstance(t, int) or t >= RING:
                    act.wait_ge(s_u, (t - RING + 1) * HALVES)
                nc.scalar.activation(at_hi[:, j, :, :], ta_ps[:].rearrange("p (k b) -> p k b", k=KT),
                                     ACT.Copy).then_inc(s_athi, 1)
                nc.scalar.activation(at_xy[:, j, :, :], t5_ps[:, 0:2 * NB].rearrange("p (k b) -> p k b", k=2),
                                     ACT.Copy).then_inc(s_athi, 1)

            def split_chunk(i):
                act.wait_ge(s_chunk, (i + 1) * 16)
                nc.scalar.activation(w_hi[:, bass.ds(i * CH, CH)], chunk[:], ACT.Copy).then_inc(s_chi, 1)

            for k in ORDER[:3]:
                split_tile(k)
            high_parts(0, 0)
            for k in ORDER[3:]:
                split_tile(k)
            for t in range(1, 3):
                high_parts(t % RING, t)
            split_chunk(0)
            with act.Fori(0, CHUNKS - 1) as n:
                i = n + 1
                for j in range(RING):
                    high_parts(j, i * RING + j)
                split_chunk(i)
            with act.Fori(0, T // RING - CHUNKS) as n:
                i = n + CHUNKS
                for j in range(RING):
                    high_parts(j, i * RING + j)

            act.wait_ge(s_qk, 1)
            nc.scalar.activation(qk_sb[:], pa[:, 0:D], ACT.Copy).then_inc(s_qk, 1)

            def compact(o, i):
                return nc.scalar.activation(o.rearrange("p (s t) -> p s t", t=T),
                                            i.rearrange("p (s t) -> p s t", t=TP)[:, :, 0:T], ACT.Copy)

            def act_step(g, name):
                if name == "xnT":
                    act.wait_ge(s_pe, g * 8 + 1)
                    nc.scalar.activation(xnT[:].rearrange("p a b -> p (a b)"), pa[:], ACT.Copy).then_inc(s_ac, 1)
                if name == "pT":
                    act.wait_ge(s_pe, g * 8 + 2)
                    nc.scalar.activation(pT[:].rearrange("p a b -> p (a b)"), pb[:], ACT.Copy).then_inc(s_ac, 1)
                if name == "exp":
                    act.wait_ge(s_dv, g * N_DV + DV["sub"])
                    for b in range(2):
                        v = att[b * TP:(b + 1) * TP, :, b * TP:b * TP + T]
                        nc.scalar.activation(v, v, ACT.Exp).then_inc(s_ac, 1)
                if name == "x2T":
                    act.wait_ge(s_pe, g * 8 + 6)
                    after(act, s_xlo, g)
                    compact(x2n[:], pa[:]).then_inc(s_ac, 1)
                if name == "score":
                    act.wait_ge(s_pe, g * 8 + 7)
                    nc.scalar.activation(score[0:TT, :, 0:NE],
                                         pa[0:TT, 0:PT * NE].rearrange("p (a e) -> p a e", a=PT),
                                         ACT.Copy).then_inc(s_ac, 1)
                if name == "gexp":
                    act.wait_ge(s_dv, g * N_DV + DV["gsub"])
                    nc.scalar.activation(ex[0:TT], ex[0:TT], ACT.Exp).then_inc(s_ac, 1)
                if name == "combT":
                    act.wait_ge(s_pe, g * 8 + 8)
                    after(act, s_comb, 32 * g)
                    nc.scalar.activation(combT[:].rearrange("p a t -> p (a t)"), pb[:, 0:GT // 2], ACT.Copy).then_inc(s_ac, 1)

            def y_copy(g):
                act.wait_ge(s_y, (g + 1) * NQ)
                act.wait_ge(s_fin, g + 1)
                nc.scalar.activation(yT[:].rearrange("p a b t -> p (a b) t")[:, :, 0:T],
                                     y_ps[:, 0:GT].rearrange("p (s t) -> p s t", t=T), ACT.Copy).then_inc(s_yc, 1)

            def keep(g):
                act.wait_ge(s_fin, g + 1)
                act.wait_ge(s_dv, g * N_DV + DV["h2"])
                nc.scalar.activation(h2_kept[:], h2[:], ACT.Copy).then_inc(s_kept, 1)

            def x_high(g):
                act.wait_ge(s_ac, g * 8 + AC["x2T"])
                after(act, s_x3, g * NQ)
                nc.scalar.activation(x_hi[:], x2n[:], ACT.Copy).then_inc(s_xhi, 1)

            def silu(g, q):
                n = g * NQ + q
                act.wait_ge(s_x1, n + 1)
                if q in (2, 3):
                    after(act, s_h, n - 1)
                else:
                    after(act, s_sc, g * (NQ - 2) + q - (1 if q < 2 else 3))
                nc.scalar.activation(sig[:, q % 2, :], x1_ps[:, q % 2, 0:GT], ACT.Silu).then_inc(s_silu, 1)

            def high_part(g, q):
                act.wait_ge(s_h, g * NQ + q + 1)
                after(act, s_y, last_use(HID_SLOT, g, q))
                k = HID_SLOT[q]
                nc.scalar.activation(hid_hi[:, k, :], hid[:, k, :], ACT.Copy).then_inc(s_hi, 1)

            NAMES = ("xnT", "pT", "exp", "x2T", "score", "gexp", "combT")

            def pairs(g, qs, attention=False, prev=True):
                for q in qs:
                    silu(g, q)
                    if q >= HI_LAG:
                        high_part(g, q - HI_LAG)
                    elif prev:
                        high_part(g - 1, NQ - HI_LAG + q)
                    if attention and q == NQ - 1:
                        x_high(g + 1)
                    if q == LAG - 1 and prev:
                        y_copy(g - 1)
                    if q == RUN["keep"]:
                        keep(g)
                    if attention:
                        for name in NAMES:
                            if q == RUN[name]:
                                act_step(g + 1, name)

            for name in NAMES:
                act_step(0, name)
            x_high(0)
            pairs(0, range(HEAD), prev=False)
            with act.Fori(0, NG - 1) as g:
                pairs(g, range(HEAD, NQ), attention=True)
                pairs(g + 1, range(HEAD))
            pairs(NG - 1, range(HEAD, NQ))
            for q in range(NQ - HI_LAG, NQ):
                high_part(NG - 1, q)
            y_copy(NG - 1)

        @block.vector
        def _(dve):
            pre = [0]

            def setup(ins, wait=True):
                pre[0] += 1
                ins.then_inc(s_pre, 1)
                if wait:
                    dve.wait_ge(s_pre, pre[0])

            def vec(k):
                return steps[:, :, k:k + C]

            nc.vector.memset(ws_raw[BC:P, ORDER.index(Y) % RAW, :], 0.0).then_inc(s_clear, 1)
            nc.vector.memset(slot[:], 0.0).then_inc(s_clear, 1)
            dve.wait_ge(s_in, 48)
            setup(nc.vector.tensor_tensor(vec(K_V)[:, :, 1:C], x_sb[:, 1:, :], x_sb[:, 0:T, :], ALU.subtract), False)
            setup(nc.vector.tensor_tensor(vec(K_V)[:, :, 0], t_sb[:, 1:], t_sb[:, 0:T], ALU.subtract), False)
            setup(nc.vector.tensor_tensor(s1_sb[:, :, 1:C], x_sb[:, 0:T, :],
                                          x_sb[:, 0:1, :].to_broadcast([P, T, C - 1]), ALU.subtract), False)
            setup(nc.vector.tensor_scalar(s1_sb[:, :, 0], t_sb[:, 0:T], t_sb[:, 0:1], None, ALU.subtract), False)
            setup(nc.vector.memset(steps[:, :, K_ONE], 1.0))
            setup(nc.vector.tensor_scalar(vec(K_VH), vec(K_V), 0.5, None, ALU.mult), False)
            setup(nc.vector.tensor_scalar(vec(K_VT), vec(K_V), 1.0 / 3.0, None, ALU.mult), False)
            setup(nc.vector.scalar_tensor_tensor(vec(K_E1), vec(K_V), 0.25, s1_sb[:], ALU.mult, ALU.add), False)
            setup(nc.vector.scalar_tensor_tensor(vec(K_D1), vec(K_V), 1.0 / 3.0, s1_sb[:], ALU.mult, ALU.add), False)
            setup(nc.vector.scalar_tensor_tensor(vec(K_C), vec(K_V), 0.5, s1_sb[:], ALU.mult, ALU.add))
            assert pre[0] == N_PRE
            def split_tile(k):
                n = ORDER.index(k)
                raw = ws_raw[:, n % RAW, :]
                dve.wait_ge(s_rawhi, n + 1)
                if k < KT:
                    nc.vector.tensor_tensor(ws_lo[:, k, :], raw, ws_hi[:, k, :].bitcast(F32),
                                            ALU.subtract).then_inc(s_rawlo, 1)
                else:
                    b, c = slice(0, BC), slice(BC, BC + 32)
                    nc.vector.tensor_tensor(raw[c].bitcast(F32R), raw[c], ws_xy[c, 1, :].bitcast(F32),
                                            ALU.subtract).then_inc(s_rawlo, 1)
                    nc.vector.tensor_tensor(ws_xy[b, 1, :], raw[b], ws_xy[b, 1, :].bitcast(F32),
                                            ALU.subtract).then_inc(s_rawlo, 1)

            def outer(o, a, b, na):
                nb = b.shape[-1]
                return nc.vector.tensor_tensor(
                    o.rearrange("p (a b) -> p a b", a=na),
                    a.unsqueeze(2).to_broadcast([P, na, nb]),
                    b.unsqueeze(1).to_broadcast([P, na, nb]), ALU.mult)

            def factor(j, t):
                s = slot[:, j, :]
                dve.wait_ge(s_slot, 2 * t + 2)
                outer(small[:, 2, :], s[:, O_E1:O_E1 + C], s[:, O_VT:O_VT + C], C).then_inc(s_e, 1)
                dve.wait_ge(s_e, 3 * t + 1)
                dve.wait_ge(s_s2, t + 1)
                nc.vector.tensor_tensor(small[:, 3, :], s2r[:, j, :], small[:, 2, :], ALU.add).then_inc(s_e, 1)
                dve.wait_ge(s_e, 3 * t + 2)
                outer(e3[:], small[:, 3, :], s[:, O_VH:O_VH + C], C * C).then_inc(s_e, 1)
                dve.wait_ge(s_e, 3 * t + 3)
                dve.wait_ge(s_s3, t + 1)
                after(dve, s_ta, t)
                nc.vector.tensor_tensor(a_sb[:], s3r[:, j, :], e3[:], ALU.add).then_inc(s_a, 1)

            def low_parts(j, t):
                dve.wait_ge(s_athi, 2 * (t + 1))
                nc.vector.tensor_tensor(at_lo[:, j, :, :], ta_ps[:].rearrange("p (k b) -> p k b", k=KT),
                                        at_hi[:, j, :, :].bitcast(F32), ALU.subtract).then_inc(s_atlo, 1)
                for k, r in ((0, BC), (1, BC + 2 * C1_STEP)):
                    nc.vector.tensor_tensor(at_xy[r:P, j, k, :], t5_ps[r:P, k * NB:(k + 1) * NB],
                                            at_xy[r:P, j, k, :].bitcast(F32), ALU.subtract).then_inc(s_atlo, 1)

            def tokens(i, j, t):
                after(dve, s_hst[j], 16 * i)
                for l in range(C):
                    if l % (C // HALVES) == 0:
                        dve.wait_ge(s_u, HALVES * t + l // (C // HALVES) + 1)
                    after(dve, s_acc, t * C + l)
                    prev = h_sb[:, (j - 1) % RING, :] if l == 0 else h_sb[:, j, :]
                    o = l % (C // HALVES) * D
                    nc.vector.scalar_tensor_tensor(
                        h_sb[:, j, :], u_ps[:, j, l // (C // HALVES), o:o + D],
                        slot[:, j, O_V + l:O_V + l + 1], prev, ALU.mult, ALU.add).then_inc(s_acc, 1)

            split_tile(0)
            factor(0, 0)
            split_tile(1)
            low_parts(0, 0)
            for k in (Y, 2, 3):
                split_tile(k)
            factor(1, 1)

            def body(i, j, t, last):
                if not last or j < RING - 1:
                    low_parts((j + 1) % RING, t + 1)
                if not last or j < RING - 2:
                    factor((j + 2) % RING, t + 2)
                tokens(i, j, t)

            for j in range(RING):
                body(0, j, j, False)
            with dve.Fori(0, T // RING - 2) as n:
                i = n + 1
                for j in range(RING):
                    body(i, j, i * RING + j, False)
            for j in range(RING):
                body(T // RING - 1, j, T - RING + j, True)

            dve.wait_ge(s_u, HALVES * T)
            dve.wait_ge(s_acc, C * T)
            dve.wait_ge(s_clo, CHUNKS)
            dve.wait_ge(s_s3, T + 1)
            for j in range(RING):
                dve.wait_ge(s_hst[j], 16 * (T // RING))
            nc.vector.memset(h_tok[:], 0.0)
            nc.vector.memset(att[:], 0.0)
            nc.vector.memset(yT[:], 0.0)
            nc.vector.memset(mhalf[:], -0.5).then_inc(s_yc, 1)
            nc.vector.memset(eps[:], EPS).then_inc(s_fin, 1)
            nc.vector.memset(spare[:], 0.0).then_inc(s_out, 1)
            nc.vector.memset(score[:], SENTINEL).then_inc(s_zero, 1)
            dve.wait_ge(s_zero, 1)

            def ts(o, i, a, b, op0, op1):
                return nc.vector.tensor_scalar(o, i, a, b, op0, op1)

            def norm_stats(g, src, first, base):
                for p in range(PT):
                    nc.vector.bn_stats(st[:, p, :], src[:, p, :]).then_inc(s_dv, 1)
                wait_apart(dve, s_dv, g * N_DV + base + PT, 0 if first else 1)
                for p in range(PT):
                    nc.vector.bn_aggr(mv[:, p, :], st[:, p, :]).then_inc(s_dv, 1)

            def normalise(g, src, norm):
                dve.wait_ge(s_rstd, g * 2 + norm + 1)
                for p in range(PT):
                    ts(xn[:, p, :], src[:, p, :], mv[:, p, 0:1], rstd[:, p:p + 1],
                       ALU.subtract, ALU.mult).then_inc(s_dv, 1)

            def dve_step(g, name):
                base = g * N_DV
                if name == "var1":
                    dve.wait_ge(s_load, g * 32 + 32)
                    norm_stats(g, h_tok, True, DV["var1"] - 8)
                if name == "xn1":
                    normalise(g, h_tok, 0)
                if name == "sub":
                    dve.wait_ge(s_pe, g * 8 + 4)
                    for b in range(2):
                        r = slice(b * TP, (b + 1) * TP)
                        sc = pb[r, :].rearrange("p (a q) -> p a q", a=PT)[:, :, b * TP:b * TP + T]
                        nc.vector.tensor_reduce(mx[r, :], sc, AX_X, ALU.max).then_inc(s_dv, 1)
                    for b in range(2):
                        r = slice(b * TP, (b + 1) * TP)
                        sc = pb[r, :].rearrange("p (a q) -> p a q", a=PT)[:, :, b * TP:b * TP + T]
                        dve.wait_ge(s_dv, base + DV["sub"] - 3 + b)
                        nc.vector.tensor_tensor(att[r, :, b * TP:b * TP + T], sc,
                                                mx[r, :].unsqueeze(2).to_broadcast([TP, PT, T]),
                                                ALU.subtract).then_inc(s_dv, 1)
                if name == "v":
                    dve.wait_ge(s_ac, g * 8 + AC["exp"])
                    for b in range(2):
                        r = slice(b * TP, (b + 1) * TP)
                        nc.vector.tensor_reduce(sm[r, :], att[r, :, b * TP:b * TP + T], AX_X,
                                                ALU.add).then_inc(s_dv, 1)
                    dve.wait_ge(s_dv, base + DV["v"] - 2)
                    nc.vector.reciprocal(rs[:], sm[:]).then_inc(s_dv, 1)
                    dve.wait_ge(s_dv, base + DV["v"] - 1)
                    dve.wait_ge(s_pe, g * 8 + 3)
                    nc.vector.tensor_tensor(v_sb[:], pa[:].rearrange("p (a o) -> p a o", a=PT),
                                            rs[:].unsqueeze(2).to_broadcast([P, PT, D]), ALU.mult).then_inc(s_dv, 1)
                if name == "h2":
                    dve.wait_ge(s_pe, g * 8 + 5)
                    after(dve, s_kept, g)
                    nc.vector.tensor_tensor(h2[:], pb[:].rearrange("p (a o) -> p a o", a=PT), h_tok[:],
                                            ALU.add).then_inc(s_dv, 1)
                if name == "var2":
                    dve.wait_ge(s_dv, base + DV["h2"])
                    norm_stats(g, h2, False, DV["var2"] - 8)
                if name == "xn2":
                    normalise(g, h2, 1)
                if name == "top":
                    wait_apart(dve, s_ac, g * 8 + AC["score"], 2)
                    for p in range(PT):
                        nc.vector.max(top[0:TT, p, :], score[0:TT, p, 0:NE]).then_inc(s_dv, 1)
                if name == "gsub":
                    dve.wait_ge(s_dv, base + DV["top"])
                    nc.vector.memset(top[0:TT, :, TOPK:8], SENTINEL).then_inc(s_dv, 1)
                    nc.vector.tensor_tensor(ex[0:TT], score[0:TT, :, 0:NE],
                                            top[0:TT, :, 0:1].to_broadcast([TT, PT, NE]),
                                            ALU.subtract).then_inc(s_dv, 1)
                if name == "taken":
                    wait_apart(dve, s_dv, base + DV["gsub"] - 1, 3)
                    for p in range(PT):
                        nc.vector.match_replace(taken[0:TT, p, :], top[0:TT, p, :], score[0:TT, p, :],
                                                -SENTINEL).then_inc(s_dv, 1)
                    dve.wait_ge(s_dv, base + DV["taken"] - 1)
                    nc.vector.tensor_tensor(mask[0:TT], taken[0:TT, :, 0:NE], score[0:TT, :, 0:NE],
                                            ALU.not_equal).then_inc(s_dv, 1)
                if name == "comb":
                    dve.wait_ge(s_dv, base + DV["taken"])
                    dve.wait_ge(s_ac, g * 8 + AC["gexp"])
                    k = DV["comb"]
                    nc.vector.tensor_tensor(mask[0:TT], mask[0:TT], ex[0:TT], ALU.mult).then_inc(s_dv, 1)
                    dve.wait_ge(s_dv, base + k - 3)
                    nc.vector.tensor_reduce(gsum[0:TT], mask[0:TT], AX_X, ALU.add).then_inc(s_dv, 1)
                    dve.wait_ge(s_dv, base + k - 2)
                    nc.vector.reciprocal(grs[0:TT], gsum[0:TT]).then_inc(s_dv, 1)
                    dve.wait_ge(s_dv, base + k - 1)
                    nc.vector.tensor_tensor(comb[0:TT], mask[0:TT], grs[0:TT].unsqueeze(2).to_broadcast([TT, PT, NE]),
                                            ALU.mult).then_inc(s_dv, 1)

            NAMES = ("var1", "xn1", "sub", "v", "h2", "var2", "xn2", "top", "gsub", "taken", "comb")

            def x_low(g):
                dve.wait_ge(s_xhi, g + 1)
                nc.vector.tensor_tensor(x_lo[:], x2n[:], x_hi[:].bitcast(F32), ALU.subtract).then_inc(s_xlo, 1)

            def hidden(g, q):
                n = g * NQ + q
                dve.wait_ge(s_x3, n + 1)
                if q < 2:
                    dve.wait_ge(s_silu, n + 1)
                    factor = sig[:, q % 2, :]
                else:
                    dve.wait_ge(s_sc, g * (NQ - 2) + q - 1)
                    factor = scaled[:, q % 2, :]
                after(dve, s_lo, last_use(HID_SLOT, g, q))
                nc.vector.tensor_tensor(hid[:, HID_SLOT[q], :], x3_ps[:, X3_SLOT[q], 0:GT], factor,
                                        ALU.mult).then_inc(s_h, 1)

            def low_part(g, q):
                dve.wait_ge(s_hi, g * NQ + q + 1)
                k = HID_SLOT[q]
                nc.vector.tensor_tensor(hid_lo[:, k, :], hid[:, k, :], hid_hi[:, k, :].bitcast(F32),
                                        ALU.subtract).then_inc(s_lo, 1)

            def finish(g):
                dve.wait_ge(s_yt, g + 1)
                dve.wait_ge(s_kept, g + 1)
                dve.wait_ge(s_out, g * 32 + 1)
                nc.vector.tensor_tensor(y_sb[:], pa[:].rearrange("p (a o) -> p a o", a=PT), h2_kept[:],
                                        ALU.add).then_inc(s_fin, 1)

            def pairs(g, qs, attention=False, prev=True):
                for q in qs:
                    hidden(g, q)
                    if attention:
                        for name in NAMES:
                            if q == RUN[name]:
                                dve_step(g + 1, name)
                    if q >= LO_LAG:
                        low_part(g, q - LO_LAG)
                    elif prev:
                        low_part(g - 1, NQ - LO_LAG + q)
                    if attention and q == NQ - 2:
                        x_low(g + 1)
                    if q == HEAD - 1 and prev:
                        finish(g - 1)

            for name in NAMES:
                dve_step(0, name)
            x_low(0)
            pairs(0, range(HEAD), prev=False)
            with dve.Fori(0, NG - 1) as g:
                pairs(g, range(HEAD, NQ), attention=True)
                pairs(g + 1, range(HEAD))
            pairs(NG - 1, range(HEAD, NQ))
            for q in range(NQ - LO_LAG, NQ):
                low_part(NG - 1, q)
            finish(NG - 1)

        @block.tensor
        def _(pe):
            def three(o, lhs_hi, lhs_lo, rhs_hi, rhs_lo, first=True, last=True):
                nc.tensor.matmul(o, lhs_hi, rhs_hi, start=first, stop=False)
                nc.tensor.matmul(o, lhs_lo, rhs_hi, start=False, stop=False)
                return nc.tensor.matmul(o, lhs_hi, rhs_lo, start=False, stop=last)

            def transposes(j, t):
                pe.wait_ge(s_a, t + 1)
                pe.wait_ge(s_b, t + 1)
                after(pe, s_atlo, 3 * t)
                for k in range(KT):
                    nc.tensor.transpose(ta_ps[:, k * P:(k + 1) * P], a_sb[:, k * P:(k + 1) * P], ident[:])
                for k in range(2):
                    mm = nc.tensor.transpose(t5_ps[:, k * NB:(k + 1) * NB], slot[:, j, k * BC:k * BC + P], ident[:])
                mm.then_inc(s_ta, 1)

            def product(j, h, k):
                cols = slice(h * (NU // HALVES), (h + 1) * (NU // HALVES))
                o = u_ps[:, j, h, :]
                if k < KT:
                    three(o, at_hi[:, j, k, :], at_lo[:, j, k, :], ws_hi[:, k, cols], ws_lo[:, k, cols],
                          k == 0, False)
                else:
                    mm = nc.tensor.matmul(o, at_xy[:, j, k - KT, :], ws_xy[:, k - KT, cols], start=False, stop=k == Y)
                    if k == Y:
                        mm.then_inc(s_u, 1)

            def project(j, t):
                pe.wait_ge(s_atlo, 3 * (t + 1))
                if not isinstance(t, int) or t >= RING:
                    pe.wait_ge(s_acc, (t - RING + 1) * C)
                for h in range(HALVES):
                    for k in range(KT + 2):
                        product(j, h, k)

            pe.wait_ge(s_id, 2)
            transposes(0, 0)
            pe.wait_ge(s_atlo, 3)
            for k in range(KT + 2):
                if k < KT:
                    pe.wait_ge(s_rawlo, N_LO[k])
                elif k == X:
                    pe.wait_ge(s_rawhi, len(ORDER))
                else:
                    pe.wait_ge(s_move, 16)
                product(0, 0, k)
            for k in range(KT + 2):
                if k == 2:
                    transposes(1, 1)
                product(0, 1, k)
            for t in range(1, RING):
                transposes((t + 1) % RING, t + 1)
                project(t, t)
            with pe.Fori(0, T // RING - 2) as n:
                i = n + 1
                for j in range(RING):
                    transposes((j + 1) % RING, i * RING + j + 1)
                    project(j, i * RING + j)
            for t in range(T - RING, T):
                if t + 1 < T:
                    transposes((t + 1) % RING, t + 1)
                project(t % RING, t)

            pe.wait_ge(s_wqk, 64)
            pe.wait_ge(s_acc, C * T)
            nc.tensor.matmul(pa[:, 0:D], wq_sb[:], wk_sb[:], start=True, stop=True).then_inc(s_qk, 1)
            pe.wait_ge(s_qk, 2)

            def group(g, o, pairs):
                for p in range(PT):
                    lhs, rhs = pairs(p)
                    mm = nc.tensor.matmul(o[:, p, :], lhs, rhs, start=True, stop=True)
                return mm.then_inc(s_pe, 1)

            def transpose_group(src, bank):
                for p in range(PT):
                    mm = nc.tensor.transpose(bank[:, p * P:(p + 1) * P], src[:, p, :], ident[:])
                return mm

            pa3 = pa[:].rearrange("p (a q) -> p a q", a=PT)
            pb3 = pb[:].rearrange("p (a q) -> p a q", a=PT)

            def pe_step(g, name):
                base = g * N_DV
                if name == "pe_xnT":
                    pe.wait_ge(s_dv, base + DV["xn1"])
                    after(pe, s_fin, g)
                    transpose_group(xn, pa).then_inc(s_pe, 1)
                if name == "pe_pT":
                    pe.wait_ge(s_ac, g * 8 + AC["xnT"])
                    after(pe, s_ac, g * 8)
                    nc.tensor.matmul(pb[:], qk_sb[:], xnT[:].rearrange("p a b -> p (a b)"), start=True,
                                     stop=True).then_inc(s_pe, 1)
                    group(g, pa3, lambda p: (xnT[:, p, :], wv_sb[:]))
                if name == "pe_score":
                    pe.wait_ge(s_ac, g * 8 + AC["pT"])
                    group(g, pb3, lambda p: (xnT[:, p, :], pT[:, p, :]))
                if name == "pe_out":
                    pe.wait_ge(s_dv, base + DV["v"])
                    group(g, pb3, lambda p: (att[:, p, :], v_sb[:, p, :]))
                if name == "pe_x2T":
                    pe.wait_ge(s_dv, base + DV["xn2"])
                    transpose_group(xn, pa).then_inc(s_pe, 1)
                if name == "pe_gate":
                    pe.wait_ge(s_ac, g * 8 + AC["x2T"])
                    for p in range(PT):
                        mm = nc.tensor.matmul(pa[0:TT, p * NE:(p + 1) * NE], x2n[:, p * TT:(p + 1) * TT],
                                              wg_sb[:], start=True, stop=True)
                    mm.then_inc(s_pe, 1)
                if name == "pe_combT":
                    pe.wait_ge(s_dv, base + DV["comb"])
                    for a in range(PT // 2):
                        mm = nc.tensor.transpose(pb[:, a * TT:(a + 1) * TT],
                                                 comb[0:TT, 2 * a:2 * a + 2].rearrange("p a e -> p (a e)"),
                                                 ident[0:TT, 0:TT])
                    mm.then_inc(s_pe, 1)

            NAMES = ("pe_xnT", "pe_pT", "pe_score", "pe_out", "pe_x2T", "pe_gate", "pe_combT")

            def w(kind, q, part):
                c = (kind * NQ + q) * P
                return part[:, c:c + P]

            def x1_hi(g, q):
                after(pe, s_silu, g * NQ + q - 1)
                o = x1_ps[:, q % 2, 0:GT]
                nc.tensor.matmul(o, w(0, q, w_hi), x_hi[:], start=True, stop=False)
                nc.tensor.matmul(o, w(0, q, w_lo), x_hi[:], start=False, stop=False)

            def x3_hi(g, q):
                after(pe, s_h, last_use(X3_SLOT, g, q))
                o = x3_ps[:, X3_SLOT[q], 0:GT]
                nc.tensor.matmul(o, w(1, q, w_hi), x_hi[:], start=True, stop=False)
                nc.tensor.matmul(o, w(1, q, w_lo), x_hi[:], start=False, stop=False)

            def x1_lo(g, q):
                nc.tensor.matmul(x1_ps[:, q % 2, 0:GT], w(0, q, w_hi), x_lo[:], start=False,
                                 stop=True).then_inc(s_x1, 1)

            def x3_lo(g, q):
                nc.tensor.matmul(x3_ps[:, X3_SLOT[q], 0:GT], w(1, q, w_hi), x_lo[:], start=False,
                                 stop=True).then_inc(s_x3, 1)

            def up(g, q):
                if q == 0:
                    pe.wait_ge(s_xhi, g + 1)
                    x1_hi(g, q)
                    x3_hi(g, q)
                    pe.wait_ge(s_xlo, g + 1)
                    x1_lo(g, q)
                    x3_lo(g, q)
                else:
                    x1_hi(g, q)
                    x1_lo(g, q)
                    x3_hi(g, q)
                    x3_lo(g, q)

            def down(g, q):
                n = g * NQ + q
                k = HID_SLOT[q]
                o = y_ps[:, 0:GT]
                pe.wait_ge(s_hi, n + 1)
                if q == 0:
                    pe.wait_ge(s_yc, g + 1)
                nc.tensor.matmul(o, w(2, q, w_hi), hid_hi[:, k, :], start=q == 0, stop=False)
                nc.tensor.matmul(o, w(2, q, w_lo), hid_hi[:, k, :], start=False, stop=False)
                pe.wait_ge(s_lo, n + 1)
                nc.tensor.matmul(o, w(2, q, w_hi), hid_lo[:, k, :], start=False, stop=q == NQ - 1).then_inc(s_y, 1)

            def y_transpose(g):
                pe.wait_ge(s_yc, g + 2)
                for p in range(PT):
                    mm = nc.tensor.transpose(pa[:, p * D:(p + 1) * D], yT[:, p].rearrange("p b t -> p (b t)"),
                                             ident[:])
                mm.then_inc(s_yt, 1)

            def pairs(g, qs, attention=False, prev=True):
                for q in qs:
                    if q == 0 and prev:
                        down(g - 1, NQ - LAG)
                    up(g, q)
                    if q >= LAG:
                        down(g, q - LAG)
                    elif q > 0 and prev:
                        down(g - 1, NQ - LAG + q)
                    if q == HEAD - 2 and prev:
                        pe.wait_ge(s_ac, g * 8 + AC["score"])
                        y_transpose(g - 1)
                    if attention:
                        for name in NAMES:
                            if q == RUN[name]:
                                pe_step(g + 1, name)

            for name in NAMES:
                pe_step(0, name)
            pe.wait_ge(s_clo, CHUNKS)
            pairs(0, range(HEAD), prev=False)
            with pe.Fori(0, NG - 1) as g:
                pairs(g, range(HEAD, NQ), attention=True)
                pairs(g + 1, range(HEAD))
            pairs(NG - 1, range(HEAD, NQ))
            for q in range(NQ - LAG, NQ):
                down(NG - 1, q)
            y_transpose(NG - 1)


HID_SLOTS = 5
HID_SLOT = [q % HID_SLOTS for q in range(NQ)]
X3_SLOT = [q % 3 for q in range(NQ - 1)] + [1]
HI_LAG, LO_LAG = 2, 1
N_PRE = 10
DV = {}
_n = 0
for _name, _ops in (("var1", 8), ("xn1", 4), ("sub", 4), ("v", 4), ("h2", 1), ("var2", 8), ("xn2", 4),
                    ("top", 4), ("gsub", 2), ("taken", 5), ("comb", 4)):
    _n += _ops
    DV[_name] = _n
N_DV = _n
AC = {"xnT": 1, "pT": 2, "exp": 4, "x2T": 5, "score": 6, "gexp": 7, "combT": 8}
RUN = {"keep": 8, "var1": 7, "rstd1": 8, "xn1": 9, "pe_xnT": 11, "xnT": 11, "pe_pT": 12, "pT": 12,
       "pe_score": 13, "sub": 13, "exp": 15, "v": 15, "pe_out": 17, "h2": 17, "var2": 18, "rstd2": 19,
       "xn2": 20, "pe_x2T": 22, "x2T": 22, "pe_gate": 23, "score": 23, "top": 23, "gsub": 24, "taken": 25,
       "gexp": 26, "comb": 26, "pe_combT": 29, "combT": 29}


def kernel(x, L0_tok_W, L0_tok_b, L0_attn_Wq, L0_attn_Wk, L0_attn_Wv, L0_ffn_w_gate, L0_ffn_w1, L0_ffn_w2,
           L0_ffn_w3, L0_ffn_w_sg, L0_ffn_w_su, L0_ffn_w_sd):
    import numpy as np
    import concourse.bacc as bacc
    from concourse.bass_utils import run_bass_kernel_spmd

    ffw = np.concatenate([
        np.transpose(L0_ffn_w_sg), np.transpose(L0_ffn_w1, (2, 0, 1)).reshape(D, -1),
        np.transpose(L0_ffn_w_su), np.transpose(L0_ffn_w3, (2, 0, 1)).reshape(D, -1),
        np.transpose(np.concatenate([np.transpose(L0_ffn_w_sd), np.asarray(L0_ffn_w2).reshape(-1, D)])
                     .reshape(NQ, P, D), (1, 0, 2)).reshape(P, -1)], axis=1)
    arrays = {
        "x": np.asarray(x).reshape(NB, -1),
        "tgrid": np.linspace(0.0, 1.0, T + 1, dtype=np.float32).reshape(1, -1),
        "wt": np.transpose(L0_tok_W), "bias": np.asarray(L0_tok_b).reshape(1, -1),
        "wq": L0_attn_Wq, "wk": L0_attn_Wk, "wvt": np.transpose(L0_attn_Wv),
        "wgt": np.transpose(L0_ffn_w_gate), "ffw": ffw}
    arrays = {k: np.ascontiguousarray(a) for k, a in arrays.items()}
    nc = bacc.Bacc("TRN2", target_bir_lowering=False, num_devices=1)
    args = [nc.dram_tensor(k, a.shape, mybir.dt.from_np(a.dtype), kind="ExternalInput").ap()
            for k, a in arrays.items()]
    out = nc.dram_tensor("out", (NB * T, D), F32, kind="ExternalOutput").ap()
    audio_tower(nc, *args, out)
    r = run_bass_kernel_spmd(nc, [arrays], core_ids=[0])
    return r.results[0]["out"].reshape(NB, T, D)
```
